# Optimizing a Trainium2 kernel written in Bass

```python
import numpy as np
import jax
import jax.numpy as jnp

def _softmax(x, axis=-1):
    return jax.nn.softmax(x, axis=axis)

def _gelu(x):
    return jax.nn.gelu(x, approximate=True)

def _silu(x):
    return jax.nn.silu(x)

def _sigmoid(x):
    return jax.nn.sigmoid(x)

def _layernorm(x, axis=-1, eps=1e-05):
    m = jnp.mean(x, axis=axis, keepdims=True)
    v = jnp.var(x, axis=axis, keepdims=True)
    return (x - m) / jnp.sqrt(v + eps)

def _scatter_add(tgt, idx, src, axis=0):
    return tgt.at[idx].add(src)

def _segment_sum(src, seg, n):
    return jax.ops.segment_sum(src, seg, n)
kernel_name = 'mk_adj_preln_d2_adj_r2_905e27'

def setup_inputs(seed: int=0):
    np.random.seed(seed)
    _w = jnp.asarray

    def _rec_inputs():
        import jax
        import jax.numpy as jnp
        _gk = jax.random.key(seed)
        x = -0.0002928 + 1 * jax.random.normal(jax.random.fold_in(_gk, 1), (3327, 256), jnp.float32)
        _w = (1.0 + jnp.arange(3327, dtype=jnp.float32)) ** (-0.5)
        _w = _w / _w.mean()
        _pij = jnp.clip(0.00240457 * _w[:, None] * _w[None, :], 0.0, 1.0)
        _a = jax.random.uniform(jax.random.fold_in(_gk, 2), (3327, 3327)) < _pij
        _a = jnp.logical_or(_a, jnp.eye(3327, dtype=bool))
        _af = _a.astype(jnp.float32)
        adj = _af
        return (x, adj)
    x, adj = _rec_inputs()

    def _L0_gnn_setup():
        import jax, jax.numpy as jnp
        import numpy as np
        N = 4096
        F_IN = 256
        F_OUT = 256
        DENSITY = 0.01
        key = jax.random.key(seed)
        k_x, k_adj, k_w, k_b = jax.random.split(key, 4)
        input_features = jax.random.normal(k_x, (N, F_IN), dtype=jnp.float32)
        adj = (jax.random.uniform(k_adj, (N, N)) < DENSITY).astype(jnp.float32)
        idx = jnp.arange(N)
        adj = adj.at[idx, idx].set(1.0)
        W = jax.random.normal(k_w, (F_IN, F_OUT), dtype=jnp.float32) / np.sqrt(F_IN)
        b = jax.random.normal(k_b, (F_OUT,), dtype=jnp.float32) * 0.01
        return {'input_features': input_features, 'adj': adj, 'W': W, 'b': b}
    _L0_gnn_all = _L0_gnn_setup()
    _L0_gnn_in = {k: v for k, v in _L0_gnn_all.items() if k in ('W', 'b')}
    del _L0_gnn_all

    def _L1_gnn_setup():
        import jax, jax.numpy as jnp
        import numpy as np
        N, D_IN, D_ATTN, STEPS, P_NUC, TAU = (2048, 256, 64, 2, 0.9, 1.0)
        LN_EPS = 1e-05

        def _xavier(key, shape):
            fan_in, fan_out = (shape[-2], shape[-1])
            lim = np.sqrt(6.0 / (fan_in + fan_out))
            return jax.random.uniform(key, shape, jnp.float32, -lim, lim)

        def _adj_from_feats(Xa, W1, W2, W3):
            Q = Xa @ W1
            K = Xa @ W3
            logits = Q @ W2 @ K.T / TAU
            idx = jnp.argsort(-logits, axis=1)
            vals = jnp.take_along_axis(logits, idx, axis=1)
            csum = jnp.cumsum(jax.nn.softmax(vals, axis=1), axis=1)
            k_i = jnp.sum(csum < P_NUC, axis=1) + 1
            ranks = jnp.arange(logits.shape[1])[None, :]
            keep_sorted = ranks < k_i[:, None]
            inv = jnp.argsort(idx, axis=1)
            keep = jnp.take_along_axis(keep_sorted, inv, axis=1)
            masked = jnp.where(keep, logits, -jnp.inf)
            return jax.nn.softmax(masked, axis=1)
        key = jax.random.key(seed)
        ks = jax.random.split(key, 9)
        return {'X': jax.random.normal(ks[0], (N, D_IN), jnp.float32), 'S': jax.random.uniform(ks[1], (N, N), jnp.float32), 'W1': _xavier(ks[2], (D_IN, D_ATTN)), 'W2': _xavier(ks[3], (D_ATTN, D_ATTN)), 'W3': _xavier(ks[4], (D_IN, D_ATTN)), 'U1': _xavier(ks[5], (STEPS, D_IN, D_IN)), 'U2': _xavier(ks[6], (STEPS, D_IN, D_IN)), 'U3': _xavier(ks[7], (STEPS, D_IN, D_IN)), 'gamma': jnp.ones((D_IN,), jnp.float32), 'beta': jnp.zeros((D_IN,), jnp.float32)}
    _L1_gnn_all = _L1_gnn_setup()
    _L1_gnn_in = {k: v for k, v in _L1_gnn_all.items() if k in ('W1', 'W2', 'W3', 'U1', 'U2', 'U3', 'gamma', 'beta')}
    del _L1_gnn_all
    return {'x': x, 'adj': adj, 'L0_gnn_W': _L0_gnn_in['W'], 'L0_gnn_b': _L0_gnn_in['b'], 'L1_gnn_W1': _L1_gnn_in['W1'], 'L1_gnn_W2': _L1_gnn_in['W2'], 'L1_gnn_W3': _L1_gnn_in['W3'], 'L1_gnn_U1': _L1_gnn_in['U1'], 'L1_gnn_U2': _L1_gnn_in['U2'], 'L1_gnn_U3': _L1_gnn_in['U3'], 'L1_gnn_gamma': _L1_gnn_in['gamma'], 'L1_gnn_beta': _L1_gnn_in['beta']}

def reference(x, adj, L0_gnn_W, L0_gnn_b, L1_gnn_W1, L1_gnn_W2, L1_gnn_W3, L1_gnn_U1, L1_gnn_U2, L1_gnn_U3, L1_gnn_gamma, L1_gnn_beta):
    import jax
    import jax.numpy as jnp

    def _L0_gnn_ref(input_features, adj, W, b):
        import jax, jax.numpy as jnp
        import numpy as np
        N = 4096
        F_IN = 256
        F_OUT = 256
        DENSITY = 0.01
        A = (adj != 0).astype(input_features.dtype)
        hidden = input_features @ W + b
        deg = jnp.sum(A, axis=0)
        return A @ hidden / deg[:, None]

    def _L1_gnn_ref(X, S, W1, W2, W3, U1, U2, U3, gamma, beta):
        import jax, jax.numpy as jnp
        import numpy as np
        N, D_IN, D_ATTN, STEPS, P_NUC, TAU = (2048, 256, 64, 2, 0.9, 1.0)
        LN_EPS = 1e-05

        def _xavier(key, shape):
            fan_in, fan_out = (shape[-2], shape[-1])
            lim = np.sqrt(6.0 / (fan_in + fan_out))
            return jax.random.uniform(key, shape, jnp.float32, -lim, lim)

        def _adj_from_feats(Xa, W1, W2, W3):
            Q = Xa @ W1
            K = Xa @ W3
            logits = Q @ W2 @ K.T / TAU
            idx = jnp.argsort(-logits, axis=1)
            vals = jnp.take_along_axis(logits, idx, axis=1)
            csum = jnp.cumsum(jax.nn.softmax(vals, axis=1), axis=1)
            k_i = jnp.sum(csum < P_NUC, axis=1) + 1
            ranks = jnp.arange(logits.shape[1])[None, :]
            keep_sorted = ranks < k_i[:, None]
            inv = jnp.argsort(idx, axis=1)
            keep = jnp.take_along_axis(keep_sorted, inv, axis=1)
            masked = jnp.where(keep, logits, -jnp.inf)
            return jax.nn.softmax(masked, axis=1)
        n = X.shape[0]
        S = S + jnp.eye(n, dtype=X.dtype)
        Rf = S / jnp.clip(S.sum(axis=1, keepdims=True), 1e-12)
        Rb = S / jnp.clip(S.sum(axis=0), 1e-12)[:, None]
        Xf, Xb, Xa = (X, X, X)
        Z = jnp.zeros_like(X)
        for s in range(STEPS):
            A = _adj_from_feats(Xa, W1, W2, W3)
            Xf = Rf @ Xf
            Xb = Rb @ Xb
            Xa = A @ Xa
            Z = Z + (Xf @ U1[s] + Xb @ U2[s] + Xa @ U3[s])
        Y = X + Z
        mu = Y.mean(axis=-1, keepdims=True)
        var = Y.var(axis=-1, keepdims=True)
        return (Y - mu) / jnp.sqrt(var + LN_EPS) * gamma + beta
    h = jnp.maximum(_layernorm(x, axis=-1), 0.0)
    x = x + _L0_gnn_ref(h, adj, L0_gnn_W, L0_gnn_b)
    h = jnp.maximum(_layernorm(x, axis=-1), 0.0)
    x = x + _L1_gnn_ref(h, adj, L1_gnn_W1, L1_gnn_W2, L1_gnn_W3, L1_gnn_U1, L1_gnn_U2, L1_gnn_U3, L1_gnn_gamma, L1_gnn_beta)
    return x

_drawn_inputs = setup_inputs


def setup_inputs(seed=0):
    import zlib

    import numpy as np

    out = dict(_drawn_inputs(seed))
    spreads = {'L1_gnn_gamma': (1.0, 0.2), 'L1_gnn_beta': (0.0, 0.1)}
    factors = {'L0_gnn_b': 4.81}
    for name, (base, spread) in spreads.items():
        noise = np.random.default_rng([zlib.crc32(name.encode()), seed]).standard_normal(out[name].shape)
        drawn = base * np.exp(spread * noise) if base else spread * noise
        out[name] = jnp.asarray(drawn.astype(out[name].dtype))
    for name, factor in factors.items():
        out[name] = (out[name] * factor).astype(out[name].dtype)
    return out
```

```python
import concourse.bass as bass
from concourse import mybir
from contextlib import ExitStack

FP32 = mybir.dt.float32
BF16 = mybir.dt.bfloat16
FP16 = mybir.dt.float16
I32 = mybir.dt.int32
ALU = mybir.AluOpType
ACT = mybir.ActivationFunctionType
AX = mybir.AxisListType

P = 128
N = 3327
D = 256
DA = 64
DC = D // P
NT = (N + P - 1) // P
NP = NT * P
TAIL = N - (NT - 1) * P
EPS = 1e-5
NUCLEUS = 0.9
DMA = 16

TOP = (127 << 23) + 128
LEAST_SHARE = 0.09 / N
GRAIN = 1 << 20
ROUNDS = (9, 12)
ROUNDS_SCALAR = (3, 4)
ROUNDS_BEFORE_NEXT = (3, 3)
WIDTHS = max(ROUNDS) + 1

CHUNK = 1024
LOGIT_CHUNKS = [(c, min(CHUNK, NP - c)) for c in range(0, NP, CHUNK)]
NL = len(LOGIT_CHUNKS)
FLIP_ADJ = 8
ADJ_GROUPS = [(k, min(FLIP_ADJ, NT - k)) for k in range(0, NT, FLIP_ADJ)]
NA = len(ADJ_GROUPS)
FLIP_P = 4
P_GROUPS = [(k, min(FLIP_P, NT - k)) for k in range(0, NT, FLIP_P)]
NG = len(P_GROUPS)


def graph_layers(nc, x, adj, w0, b0, w1, w2, w3, u1, u2, u3, gamma, beta, out):
    ctx = ExitStack()
    with ctx:
        def sb(name, shape, dt=FP32):
            return ctx.enter_context(nc.sbuf_tensor(name, shape, dt))

        def sem(name):
            return ctx.enter_context(nc.semaphore(name))

        s_dram = nc.dram_tensor("s_scratch", [NT, P, NP], BF16, kind="Internal").ap()
        x1_dram = nc.dram_tensor("x1_scratch", [P, NT * D], FP32, kind="Internal").ap()
        xa_dram = nc.dram_tensor("xa_scratch", [NT, P, D], FP32, kind="Internal").ap()
        y_dram = nc.dram_tensor("y_scratch", [NT, P, D], FP32, kind="Internal").ap()

        xcur = sb("xcur", [P, NT, D])
        parts = sb("parts", [P, NT, 2, D], FP16)
        both = sb("both", [P, NT, 2, 2 * D], FP16)
        q_t = sb("q_t", [P, NP])
        k_t = sb("k_t", [P, NP])
        y_all = parts[:, :, :, :].rearrange("p t a d -> p (t a d)").bitcast(FP32).rearrange("p (t d) -> p t d", t=NT)
        x1_all = both[:, 0:NT // 2, :, :].rearrange("p t a d -> p (t a d)").bitcast(FP32).rearrange(
            "p (t d) -> p t d", t=NT)
        expo = [sb(f"expo{b}", [P, NP]) for b in range(2)]
        natural = [expo[b][:, 0:NP // 2].bitcast(BF16) for b in range(2)]
        window = sb("window", [P, NP + 8])
        flipped = [sb(f"flipped{b}", [P, FLIP_P * P]) for b in range(2)]
        s_tile = [sb(f"s_tile{b}", [P, NT, P], BF16) for b in range(2)]
        q_tile = [sb(f"q_tile{b}", [P, P]) for b in range(2)]
        ht = [sb(f"ht{b}", [P, D]) for b in range(2)]
        xfb = sb("xfb", [P, 2 * D])
        turned = sb("turned", [P, (3 * DC + 1) * P])
        xfbt = turned[:, 0:2 * DC * P].rearrange("p (c i) -> p c i", c=2 * DC)
        xt = turned[:, 2 * DC * P:3 * DC * P].rearrange("p (c i) -> p c i", c=DC)
        unused = turned[:, :].bitcast(mybir.dt.uint8)[:, 0:N]
        y_tile = sb("y_tile", [P, D])
        y_in = y_tile
        qraw = sb("qraw", [DA, P])
        w0_sb = flipped[0][:, :].rearrange("p (c n) -> p c n", c=DC)
        b0_sb = flipped[1][:, 0:D]
        w1_sb = sb("w1_sb", [P, DC, DA])
        w3_sb = sb("w3_sb", [P, DC, 2, DA])
        w2_sb = sb("w2_sb", [DA, 2, DA])
        u_sb = sb("u_sb", [P, 3, DC, D])
        gamma_sb = u_sb[:, 0, 0, :]
        beta_sb = u_sb[:, 0, 1, :]
        ident = sb("ident", [P, P])
        ident_bf = sb("ident_bf", [P, P], BF16)
        ones_bf = sb("ones_bf", [P, 1], BF16)
        zeros_bf = sb("zeros_bf", [P, P], BF16)
        ones8 = sb("ones8", [P, 8])
        stats6 = sb("stats6", [P, 6])
        stats2 = sb("stats2", [P, 2])
        mean = sb("mean", [P, NT])
        var = sb("var", [P, NT])
        rstd = sb("rstd", [P, NT])
        row_n = sb("row_n", [P, NT])
        col_n = sb("col_n", [P, NT])
        deg_inv = sb("deg_inv", [P, NT])
        row_inv = sb("row_inv", [P, NT])
        col_inv = sb("col_inv", [P, NT])
        maxes = sb("maxes", [P, NL])
        neg_max = [sb(f"neg_max{b}", [P, 1]) for b in range(2)]
        total = [sb(f"total{b}", [P, 1]) for b in range(2)]
        kept_inv = [sb(f"kept_inv{b}", [P, 1]) for b in range(2)]
        target = [sb(f"target{b}", [P, 1]) for b in range(2)]
        neg_target = [sb(f"neg_target{b}", [P, 1]) for b in range(2)]
        width = [sb(f"width{b}", [P, WIDTHS]) for b in range(2)]
        halves = sb("halves", [P, WIDTHS])
        neg_cut = sb("neg_cut", [P, 1])
        signs = sb("signs", [P, 1])
        excess = sb("excess", [P, 1])
        low = sb("low", [P, 1])
        span_n = sb("span_n", [P, 1], I32)
        span = sb("span", [P, 1])
        half_count = sb("half_count", [P, 1])
        side = sb("side", [P, 1])
        mass = sb("mass", [P, 1])
        move = sb("move", [P, 1])
        cut = [sb(f"cut{b}", [P, 1], I32) for b in range(2)]
        top8 = sb("top8", [P, 8])
        csum = sb("csum", [P, 9])
        keep8 = sb("keep8", [P, 8])
        edge = sb("edge", [P, 7])
        pick = sb("pick", [P, 8])
        least = sb("least", [P, 1])
        real_row = sb("real_row", [P, 1])
        top = sb("top", [P, 1])
        kept = sb("kept", [P, 1])
        below = sb("below", [P, 1])
        odd = sb("odd", [P, 32])
        odd_t = sb("odd_t", [P, 32])
        odd_q = sb("odd_q", [P, 1])
        odd4 = sb("odd4", [1, 4])
        odd_n = sb("odd_n", [1, 1], I32)

        bank = [ctx.enter_context(nc.psum_tensor(f"bank{i}", [P, 512], FP32)) for i in range(4)]
        lg = [ctx.enter_context(nc.psum_tensor(f"lg{i}", [P, CHUNK], FP32)) for i in range(2)]
        flip_ps = bank[0:2]
        pv_ps = bank[2]
        s_ps = bank[3]

        x_in = sem("x_in")
        weights_in = sem("weights_in")
        x1_stored = sem("x1_stored")
        xa_in = sem("xa_in")
        x1_in = sem("x1_in")
        out_done = sem("out_done")
        x_pad = sem("x_pad")
        consts_ready = sem("consts_ready")
        var_ready = sem("var_ready")
        std_ready = sem("std_ready")
        h_ready = sem("h_ready")
        cols_done = sem("cols_done")
        x1_ready = sem("x1_ready")
        second_ready = sem("second_ready")
        y_norm = sem("y_norm")
        conv_done = sem("conv_done")
        conv_turned = sem("conv_turned")
        conv_turned_out = sem("conv_turned_out")
        proj_done = sem("proj_done")
        s_made = sem("s_made")
        tile_ready = sem("tile_ready")
        first_x = sem("first_x")
        first_qk_step = sem("first_qk_step")
        nat_in = [sem(f"nat_in_{n}") for n in range(2)]
        s_stored = [sem(f"s_stored_{n}") for n in range(2)]
        adj_flipped = sem("adj_flipped")
        adj_moved_v = sem("adj_moved_v")
        adj_moved_s = sem("adj_moved_s")
        conv_out = sem("conv_out")
        proj_out = sem("proj_out")
        first_turned = sem("first_turned")
        first_qk_out = sem("first_qk_out")
        q_ready = [sem(f"q_ready_{n}") for n in range(2)]
        logits_ready = [sem(f"logits_ready_{n}") for n in range(2)]
        logits_copied = [sem(f"logits_copied_{n}") for n in range(2)]
        expo_ready = [sem(f"expo_ready_{n}") for n in range(2)]
        probs_ready = [sem(f"probs_ready_{n}") for n in range(2)]
        p_moved = [sem(f"p_moved_{n}") for n in range(2)]
        p_used = [sem(f"p_used_{n}") for n in range(2)]
        pv_done = [sem(f"pv_done_{n}") for n in range(2)]
        fb_t_ready = [sem(f"fb_t_ready_{n}") for n in range(2)]
        x_turned = [sem(f"x_turned_{n}") for n in range(2)]
        x_t_ready = [sem(f"x_t_ready_{n}") for n in range(2)]
        qk_step = [sem(f"qk_step_{n}") for n in range(2)]
        u_in = [sem(f"u_in_{n}") for n in range(2)]
        s_in = [[sem(f"s_in_{n}_{b}") for b in range(2)] for n in range(2)]
        xa_stored = [[sem(f"xa_stored_{n}_{b}") for b in range(2)] for n in range(2)]
        y_stored = [sem(f"y_stored_{n}") for n in range(2)]
        y_loaded = [sem(f"y_loaded_{n}") for n in range(2)]
        s_done = [sem(f"s_done_{n}") for n in range(2)]
        fb_ready = [sem(f"fb_ready_{n}") for n in range(2)]
        fb_turned = [sem(f"fb_turned_{n}") for n in range(2)]
        lo_ready = [sem(f"lo_ready_{n}") for n in range(2)]
        logits_used = [sem(f"logits_used_{n}") for n in range(2)]
        p_flipped = [sem(f"p_flipped_{n}") for n in range(2)]
        xa_ready = [sem(f"xa_ready_{n}") for n in range(2)]
        y_out = [sem(f"y_out_{n}") for n in range(2)]
        y_done = [sem(f"y_done_{n}") for n in range(2)]
        qk_out = [sem(f"qk_out_{n}") for n in range(2)]
        free_slots = [
            *[(s_stored[n], DMA) for n in range(2)],
            (adj_flipped, 8),
            (adj_moved_v, 1),
            (adj_moved_s, 1),
            (conv_out, 1),
            (proj_out, 1),
            (first_turned, 2),
            (first_qk_out, 2),
            *[(xa_stored[n][b], DMA) for n in range(2) for b in range(2)],
            *[(y_stored[n], DMA) for n in range(2)],
            *[(s_done[n], 2) for n in range(2)],
            *[(fb_ready[n], 1) for n in range(2)],
            *[(fb_turned[n], 1) for n in range(2)],
            *[(lo_ready[n], 1) for n in range(2)],
            *[(logits_used[n], 2) for n in range(2)],
            *[(p_flipped[n], 1) for n in range(2)],
            *[(xa_ready[n], 2) for n in range(2)],
            *[(y_out[n], 1) for n in range(2)],
            *[(y_done[n], 1) for n in range(2)],
            *[(qk_out[n], 2) for n in range(2)],
        ]

        V, A, G, T = nc.vector, nc.scalar, nc.gpsimd, nc.tensor

        def tiles_loop(eng, body):
            with eng.Fori(0, NT // 2 - 1) as i:
                for b in range(2):
                    body(i * 2 + b, i, b)
            for b in range(2):
                body(NT - 2 + b, NT // 2 - 1, b)

        def is_last(t):
            return isinstance(t, int) and t == NT - 1

        def tile3(buf, t):
            return buf[:, t, :] if isinstance(t, int) else buf[:, bass.ds(t, 1), :].rearrange("p a d -> p (a d)")

        def tile4(buf, t, part):
            if isinstance(t, int):
                return buf[:, t, part, :]
            return buf[:, bass.ds(t, 1), part:part + 1, :].rearrange("p a q d -> p (a q d)")

        def dram_tile(buf, t):
            return buf[t] if isinstance(t, int) else buf[bass.ds(t, 1)].rearrange("a p n -> (a p) n")

        def flat(ap):
            return ap.rearrange("p a b -> p (a b)")

        block = ctx.enter_context(nc.Block())

        @block.sync
        def _(sp):
            def spread(v):
                return v.rearrange("(a n) -> a n", a=1).broadcast_to([P, D])

            sp.wait_ge(x_pad, 1)
            sp.dma_start(xcur[:, 0:NT - 1, :], x[0:(NT - 1) * P, :].rearrange("(t p) d -> p t d", p=P)).then_inc(x_in, DMA)
            sp.dma_start(xcur[0:TAIL, NT - 1, :], x[(NT - 1) * P:N, :]).then_inc(x_in, DMA)
            sp.dma_start(w0_sb[:, :, :], w0.rearrange("(c p) n -> p c n", p=P)).then_inc(weights_in, DMA)
            sp.dma_start(b0_sb[:, :], spread(b0)).then_inc(weights_in, DMA)
            sp.dma_start(w1_sb[:, :, :], w1.rearrange("(c p) n -> p c n", p=P)).then_inc(weights_in, DMA)
            for j in range(2):
                sp.dma_start(w3_sb[:, :, j, :], w3.rearrange("(c p) n -> p c n", p=P)).then_inc(weights_in, DMA)
                sp.dma_start(w2_sb[:, j, :], w2).then_inc(weights_in, DMA)

            def load_u(s):
                for j, u in enumerate((u1, u2, u3)):
                    sp.dma_start(u_sb[:, j, :, :], u[s].rearrange("(c p) n -> p c n", p=P)).then_inc(u_in[s], DMA)
            load_u(0)

            def store_s(t, m, b):
                sp.wait_ge(s_made, t + 1)
                sp.dma_start(dram_tile(s_dram, t), flat(s_tile[b][:, :, :])).then_inc(s_stored[b], DMA)
            tiles_loop(sp, store_s)
            sp.wait_ge(x1_ready, 1)
            sp.dma_start(x1_dram, flat(x1_all)).then_inc(x1_stored, DMA)
            for b in range(2):
                sp.wait_ge(s_stored[b], DMA * (NT // 2 + 1))

            for s in range(2):
                def load(t, m, b):
                    sp.wait_ge(s_done[s], t + 1)
                    sp.dma_start(flat(s_tile[b][:, :, :]), dram_tile(s_dram, t)).then_inc(s_in[s][b], DMA)
                    if s == 1:
                        sp.wait_ge(y_done[1], t + 1)
                        sp.dma_start(y_in[:, :], dram_tile(y_dram, t)).then_inc(y_loaded[1], DMA)
                tiles_loop(sp, load)
                if s == 0:
                    for b in range(2):
                        sp.wait_ge(xa_stored[0][b], DMA * (NT // 2 + 1))
                    sp.wait_ge(y_stored[0], DMA * (NT + 1))
                    sp.wait_ge(y_done[0], NT + 1)
                    sp.dma_start(xcur[:, :, :], xa_dram.rearrange("t p d -> p t d")).then_inc(xa_in, DMA)
                    load_u(1)
            sp.wait_ge(y_done[1], NT + 1)
            sp.dma_start(flat(xcur[:, :, :]), x1_dram).then_inc(x1_in, DMA)
            sp.dma_start(gamma_sb, spread(gamma)).then_inc(x1_in, DMA)
            sp.dma_start(beta_sb, spread(beta)).then_inc(x1_in, DMA)
            sp.wait_ge(y_norm, 1)
            sp.dma_start(out[0:(NT - 1) * P, :].rearrange("(t p) d -> p t d", p=P), xcur[:, 0:NT - 1, :]).then_inc(out_done, DMA)
            sp.dma_start(out[(NT - 1) * P:N, :], xcur[0:TAIL, NT - 1, :]).then_inc(out_done, DMA)
            sp.wait_ge(out_done, DMA * 2)

        @block.gpsimd
        def _(pool):
            for m in (ident, ident_bf):
                G.memset(m[:, :], 0.0)
            pool.drain()
            for m in (ident, ident_bf):
                G.affine_select(out=m[:, :], in_=m[:, :], compare_op=ALU.not_equal, fill=1.0, base=0,
                                pattern=[[-1, P]], channel_multiplier=1)
            G.memset(ones_bf[:, :], 1.0)
            G.memset(zeros_bf[:, :], 0.0)
            G.memset(ones8[:, :], 1.0)
            G.memset(odd[:, :], 0.0)
            for r in range(WIDTHS):
                G.memset(halves[:, r:r + 1], 0.5 ** r)
            for b in range(2):
                G.memset(natural[b][:, N:NP], 0.0)
            G.memset(window[:, N:NP + 8], -1.0)
            pool.drain()
            pool.nop().then_inc(consts_ready, 1)

            def load_adj(t, m, b):
                pool.wait_ge(adj_flipped, (t - 1) * NA + 8)
                pool.wait_ge(x_in, DMA * 2)
                if is_last(t):
                    G.memset(natural[b][:, :], 0.0)
                    pool.drain()
                    pool.dma_start(natural[b][0:TAIL, 0:N], adj[(NT - 1) * P:N, :]).then_inc(nat_in[b], DMA)
                else:
                    pool.dma_start(natural[b][:, 0:N], adj[bass.ds(t * P, P), :]).then_inc(nat_in[b], DMA)
            tiles_loop(pool, load_adj)

            pool.wait_ge(x1_stored, DMA)
            def low_parts(t, m, b):
                pool.wait_ge(fb_ready[0], t + 2)
                G.tensor_tensor(tile4(both, t, 1), xfb[:, :], tile4(both, t, 0), ALU.subtract).then_inc(lo_ready[0], 1)
            tiles_loop(pool, low_parts)

        @block.scalar
        def _(act):
            act.wait_ge(var_ready, 1)
            A.activation(rstd[:, :], var[:, :], ACT.Sqrt).then_inc(std_ready, 1)

            def convolve(t, m, b):
                act.wait_ge(s_stored[b], DMA * (m + 1))
                for g, (k0, n) in enumerate(ADJ_GROUPS):
                    if g % 2:
                        act.wait_ge(adj_flipped, t * NA + g + 9)
                        A.activation(flat(s_tile[b][:, k0:k0 + n, :]), flip_ps[1][:, :].bitcast(BF16)[:, 0:n * P],
                                          ACT.Copy).then_inc(adj_moved_s, 1)
                act.wait_ge(conv_done, t + 1)
                A.activation(y_tile[:, :], s_ps[:, 0:D], ACT.Copy)
                A.activation(row_n[:, bass.ds(t, 1)], s_ps[:, D:D + 1], ACT.Copy).then_inc(conv_out, 1)
                act.wait_ge(conv_turned, t + 1)
                A.activation(flat(xt[:, :, :]), pv_ps[:, 0:D], ACT.Copy).then_inc(conv_turned_out, 1)
            tiles_loop(act, convolve)
            act.wait_ge(var_ready, 2)
            A.activation(rstd[:, :], var[:, :], ACT.Sqrt).then_inc(std_ready, 1)

            def query_key(t, half, steps, outs):
                r0, r1 = DA * half, DA * (half + 1)
                act.wait_ge(steps, t * 2 + 1)
                A.activation(qraw[:, :], flip_ps[0][0:DA, 0:P], ACT.Copy)
                A.activation(k_t[r0:r1, bass.ds(t * P, P)], flip_ps[0][r0:r1, P:2 * P], ACT.Copy).then_inc(outs, 1)
                act.wait_ge(steps, t * 2 + 2)
                A.activation(q_t[r0:r1, bass.ds(t * P, P)], flip_ps[0][r0:r1, 2 * P:3 * P], ACT.Copy).then_inc(outs, 1)

            def first_query_key(t, m, b):
                act.wait_ge(first_turned, t + 3)
                A.activation(flat(xt[:, :, :]), pv_ps[:, D:2 * D], ACT.Copy).then_inc(first_x, 1)
                query_key(t, 0, first_qk_step, first_qk_out)
            tiles_loop(act, first_query_key)
            act.wait_ge(second_ready, 1)
            act.wait_ge(x1_stored, DMA)

            for s in range(2):
                act.drain()
                r0, r1 = DA * s, DA * (s + 1)

                def stage_query(t, b):
                    A.activation(q_tile[b][r0:r1, :], q_t[r0:r1, bass.ds(t * P, P)], ACT.Copy).then_inc(q_ready[s], 1)

                def exponentials(t, b):
                    act.wait_ge(logits_copied[s], t + 1)
                    A.activation(expo[b][:, 0:N], expo[b][:, 0:N], ACT.Exp, bias=neg_max[b][:, :],
                                 accum_out=total[b][:, :])
                    act.drain()
                    A.activation(low[:, :], total[b][:, :], ACT.Copy, scale=LEAST_SHARE)
                    A.activation(neg_target[b][:, :], total[b][:, :], ACT.Copy, scale=-NUCLEUS)
                    A.activation(target[b][:, :], total[b][:, :], ACT.Copy, scale=NUCLEUS)
                    act.drain()
                    A.activation(span_n[:, :], low[:, :].bitcast(I32), ACT.Copy, scale=-1.0 / GRAIN, bias=float(TOP // GRAIN + 1))
                    act.drain()
                    A.activation(span[:, :], span_n[:, :], ACT.Copy, scale=float(GRAIN))
                    act.drain()
                    A.activation(width[b][:, :], halves[:, :], ACT.Copy, scale=span[:, :])
                    A.activation(cut[b][:, :], span[:, :], ACT.Copy, scale=-0.5, bias=float(TOP))
                    for r in range(ROUNDS_SCALAR[s]):
                        act.drain()
                        A.activation(neg_cut[:, :], cut[b][:, :].bitcast(FP32), ACT.Copy, scale=-1.0)
                        act.drain()
                        A.activation(unused, expo[b][:, 0:N], ACT.Sign, bias=neg_cut[:, :],
                                     accum_out=signs[:, :])
                        act.drain()
                        A.activation(unused, expo[b][:, 0:N], ACT.Relu, bias=neg_cut[:, :],
                                     accum_out=excess[:, :])
                        act.drain()
                        A.activation(half_count[:, :], signs[:, :], ACT.Copy, scale=0.5, bias=N / 2.0)
                        act.drain()
                        A.activation(side[:, :], half_count[:, :], ACT.Identity, scale=cut[b][:, :].bitcast(FP32),
                                     bias=excess[:, :])
                        act.drain()
                        A.activation(side[:, :], side[:, :], ACT.Sign, bias=neg_target[b][:, :])
                        act.drain()
                        last = A.activation(cut[b][:, :], side[:, :], ACT.Identity, scale=width[b][:, r + 2:r + 3],
                                            bias=cut[b][:, :])
                    last.then_inc(expo_ready[s], 1)

                def step(t, m, b):
                    act.wait_ge(s_done[s], t + 3)
                    act.wait_ge(fb_turned[s], t + 1)
                    if s == 0:
                        act.wait_ge(lo_ready[0], t + 1)
                    A.activation(xfb[:, 0:D], s_ps[:, 0:D], ACT.Copy, scale=row_inv[:, bass.ds(t, 1)])
                    last = A.activation(xfb[:, D:2 * D], s_ps[:, 0:D] if s == 0 else s_ps[:, D:2 * D], ACT.Copy,
                                        scale=col_inv[:, bass.ds(t, 1)])
                    if s == 0:
                        act.drain()
                        last = A.activation(tile4(both, t, 0), xfb[:, :], ACT.Copy)
                    last.then_inc(fb_ready[s], 1)
                    if not (isinstance(t, int) and t >= NT - 2):
                        act.wait_ge(logits_ready[s], (t + 1) * NL)
                        stage_query(t + 2, b)
                    if not is_last(t):
                        exponentials(t + 1, 1 - b)
                    for g, (k0, n) in enumerate(P_GROUPS):
                        act.wait_ge(p_flipped[s], t * NG + g + 2)
                        if g >= 2:
                            act.wait_ge(p_used[s], t * (NG - 1) + g - 1)
                        A.activation(flipped[g % 2][:, 0:n * P], flip_ps[g % 2][:, 0:n * P], ACT.Copy).then_inc(p_moved[s], 1)
                    act.wait_ge(pv_done[s], t + 1)
                    if s == 0:
                        act.wait_ge(xa_stored[0][b], DMA * (m + 1))
                    A.activation(ht[b][:, :], pv_ps[:, 0:D], ACT.Copy, scale=kept_inv[b][:, :]).then_inc(xa_ready[s], 1)
                    act.wait_ge(fb_turned[s], t + 2)
                    A.activation(flat(xfbt[:, :, :]), flip_ps[1][:, :], ACT.Copy).then_inc(fb_t_ready[s], 1)
                    act.wait_ge(x_turned[s], t + 1)
                    A.activation(flat(xt[:, :, :]), pv_ps[:, D:2 * D], ACT.Copy).then_inc(x_t_ready[s], 1)
                    if s == 0:
                        query_key(t, 1, qk_step[0], qk_out[0])
                        act.wait_ge(xa_ready[0], t + 3)
                        act.dma_start(dram_tile(xa_dram, t), ht[b][:, :]).then_inc(xa_stored[0][b], DMA)
                    act.wait_ge(y_done[s], t + 2)
                    if s == 0:
                        act.wait_ge(y_stored[0], DMA * (t + 1))
                        A.activation(y_tile[:, :], pv_ps[:, 0:D], ACT.Copy).then_inc(y_out[0], 1)
                        act.wait_ge(y_out[0], t + 2)
                        act.dma_start(dram_tile(y_dram, t), y_tile[:, :]).then_inc(y_stored[0], DMA)
                    else:
                        A.activation(tile3(y_all, t), pv_ps[:, 0:D], ACT.Copy).then_inc(y_out[1], 1)
                for t in range(2):
                    stage_query(t, t)
                exponentials(0, 0)
                tiles_loop(act, step)
            act.wait_ge(var_ready, 3)
            A.activation(rstd[:, :], var[:, :], ACT.Sqrt).then_inc(std_ready, 1)

        @block.tensor
        def _(pe):
            pe.wait_ge(consts_ready, 1)
            pe.wait_ge(h_ready, 1)
            pe.wait_ge(weights_in, DMA * 7)
            T.matmul(lg[0][:, 0:NT], zeros_bf[:, :], zeros_bf[:, 0:NT], start=True, stop=True)

            def convolve(t, m, b):
                pe.wait_ge(nat_in[b], DMA * (m + 1))
                for k in range(NT):
                    T.matmul(lg[0][:, k:k + 1], natural[b][:, k * P:(k + 1) * P], ones_bf[:, :], start=False, stop=True,
                             skip_group_check=True)
                for g, (k0, n) in enumerate(ADJ_GROUPS):
                    pe.wait_ge(adj_moved_s if g % 2 else adj_moved_v, t * (NA // 2) + g // 2 + 1)
                    view = flip_ps[g % 2][:, :].bitcast(BF16)
                    for k in range(n):
                        last = T.transpose(view[:, k * P:(k + 1) * P], natural[b][:, (k0 + k) * P:(k0 + k + 1) * P],
                                           ident_bf[:, :])
                    last.then_inc(adj_flipped, 1)
                pe.wait_ge(adj_moved_v, (t + 1) * (NA // 2) + 1)
                pe.wait_ge(adj_moved_s, (t + 1) * (NA // 2) + 1)
                pe.wait_ge(conv_out, t + 1)
                for k in range(NT):
                    for part in range(2):
                        T.matmul(s_ps[:, 0:D], s_tile[b][:, k, :], parts[:, k, part, :], start=(k == 0 and part == 0),
                                 stop=(k == NT - 1 and part == 1), skip_group_check=True)
                    last = T.matmul(s_ps[:, D:D + 1], s_tile[b][:, k, :], ones_bf[:, :], start=False, stop=(k == NT - 1),
                                    skip_group_check=True)
                last.then_inc(conv_done, 1)
                pe.wait_ge(conv_out, t + 2)
                pe.wait_ge(proj_out, t + 1)
                for c in range(DC):
                    last = T.transpose(pv_ps[:, c * P:(c + 1) * P], y_tile[:, c * P:(c + 1) * P], ident[:, :])
                last.then_inc(conv_turned, 1)
                pe.wait_ge(conv_turned_out, t + 1)
                for c in range(DC):
                    last = T.matmul(pv_ps[:, D:2 * D], xt[:, c, :], w0_sb[:, c, :], start=(c == 0), stop=(c == DC - 1))
                last.then_inc(proj_done, 1)
            tiles_loop(pe, convolve)
            T.matmul(lg[0][:, 0:NT], zeros_bf[:, :], zeros_bf[:, 0:NT], start=False, stop=True, skip_group_check=True).then_inc(cols_done, 1)

            def query_key(t, half, steps, outs):
                for c in range(DC):
                    T.matmul(flip_ps[0][0:DA, 0:P], w1_sb[:, c, :], xt[:, c, :], start=(c == 0), stop=(c == DC - 1))
                for c in range(DC):
                    last = T.matmul(flip_ps[0][:, P:2 * P], flat(w3_sb[:, c, :, :]), xt[:, c, :], start=(c == 0),
                                    stop=(c == DC - 1))
                last.then_inc(steps, 1)
                pe.wait_ge(outs, t * 2 + 3)
                T.matmul(flip_ps[0][:, 2 * P:3 * P], flat(w2_sb[:, :, :]), qraw[:, :], start=True, stop=True).then_inc(steps, 1)

            def first_query_key(t, m, b):
                pe.wait_ge(tile_ready, t + 1)
                pe.wait_ge(first_qk_out, t * 2 + 2)
                for c in range(DC):
                    last = T.transpose(pv_ps[:, D + c * P:D + (c + 1) * P], ht[b][:, c * P:(c + 1) * P], ident[:, :])
                last.then_inc(first_turned, 1)
                pe.wait_ge(first_x, t + 1)
                query_key(t, 0, first_qk_step, first_qk_out)
            tiles_loop(pe, first_query_key)
            pe.wait_ge(first_qk_out, 2 * NT + 2)
            pe.wait_ge(second_ready, 1)

            for s in range(2):
                r0, r1 = DA * s, DA * (s + 1)

                def logits(t, b):
                    pe.wait_ge(q_ready[s], t + 1)
                    for c, (c0, w) in enumerate(LOGIT_CHUNKS):
                        pe.wait_ge(logits_used[s], t * NL + c + 1)
                        for c1 in range(0, w, 512):
                            n = min(512, w - c1)
                            last = T.matmul(lg[c % 2][:, c1:c1 + n], q_tile[b][r0:r1, :], k_t[r0:r1, c0 + c1:c0 + c1 + n],
                                            start=True, stop=True)
                        last.then_inc(logits_ready[s], 1)

                def step(t, m, b):
                    pe.wait_ge(s_in[s][b], DMA * (m + 1))
                    pe.wait_ge(fb_ready[s], t + 1)
                    width, src = (D, parts) if s == 0 else (2 * D, both)
                    for k in range(NT):
                        for part in range(2):
                            last = T.matmul(s_ps[:, 0:width], s_tile[b][:, k, :], src[:, k, part, :],
                                            start=(k == 0 and part == 0), stop=(k == NT - 1 and part == 1))
                    last.then_inc(s_done[s], 1)
                    pe.wait_ge(probs_ready[s], t + 1)
                    pe.wait_ge(y_out[s], t + 1)

                    def times_rows(g):
                        k0, n = P_GROUPS[g]
                        pe.wait_ge(p_moved[s], t * NG + g + 1)
                        for k in range(n):
                            last = T.matmul(pv_ps[:, 0:D], flipped[g % 2][:, k * P:(k + 1) * P], xcur[:, k0 + k, :],
                                            start=(k0 + k == 0), stop=(k0 + k == NT - 1))
                        last.then_inc(pv_done[s] if g == NG - 1 else p_used[s], 1)
                    for g, (k0, n) in enumerate(P_GROUPS):
                        if g >= 2:
                            pe.wait_ge(p_moved[s], t * NG + g - 1)
                        for k in range(n):
                            last = T.transpose(flip_ps[g % 2][:, k * P:(k + 1) * P],
                                               expo[b][:, (k0 + k) * P:(k0 + k + 1) * P], ident[:, :])
                        last.then_inc(p_flipped[s], 1)
                        if g >= 1:
                            times_rows(g - 1)
                    times_rows(NG - 1)
                    if not (isinstance(t, int) and t >= NT - 2):
                        logits(t + 2, b)
                    pe.wait_ge(fb_ready[s], t + 2)
                    for c in range(2 * DC):
                        last = T.transpose(flip_ps[1][:, c * P:(c + 1) * P], xfb[:, c * P:(c + 1) * P], ident[:, :])
                    last.then_inc(fb_turned[s], 1)
                    pe.wait_ge(xa_ready[s], t + 3)
                    for c in range(DC):
                        last = T.transpose(pv_ps[:, D + c * P:D + (c + 1) * P], ht[b][:, c * P:(c + 1) * P], ident[:, :])
                    last.then_inc(x_turned[s], 1)
                    pe.wait_ge(fb_t_ready[s], t + 1)
                    pe.wait_ge(x_t_ready[s], t + 1)
                    if s == 0:
                        query_key(t, 1, qk_step[0], qk_out[0])
                    if s == 0:
                        T.matmul(pv_ps[:, 0:D], ident[:, :], tile3(xcur, t), start=True, stop=False)
                    else:
                        pe.wait_ge(y_loaded[1], DMA * (t + 1))
                        T.matmul(pv_ps[:, 0:D], ident[:, :], y_in[:, :], start=True, stop=False)
                    for j, turned in enumerate((xfbt[:, 0:DC, :], xfbt[:, DC:2 * DC, :], xt[:, :, :])):
                        for c in range(DC):
                            last = T.matmul(pv_ps[:, 0:D], turned[:, c, :], u_sb[:, j, c, :], start=False,
                                            stop=(j == 2 and c == DC - 1))
                    last.then_inc(y_done[s], 1)
                    if s == 0:
                        pe.wait_ge(qk_out[0], (t + 1) * 2 + 2)
                if s == 1:
                    pe.wait_ge(xa_in, DMA)
                    pe.wait_ge(lo_ready[0], NT + 1)
                pe.wait_ge(u_in[s], DMA * 3)
                for t in range(2):
                    logits(t, t)
                tiles_loop(pe, step)

        @block.vector
        def _(dve):
            for slots, count in free_slots:
                dve.sem_inc(slots, count)
            V.memset(xcur[:, NT - 1, :], 0.0).then_inc(x_pad, 1)
            dve.wait_ge(x_in, DMA * 2)

            def norm_stats(src, t):
                V.bn_stats(stats6[:, :], src)
                dve.drain()
                V.bn_aggr(stats2[:, :], stats6[:, :])
                dve.drain()
                V.tensor_copy(mean[:, bass.ds(t, 1)], stats2[:, 0:1])
                V.tensor_scalar(var[:, bass.ds(t, 1)], stats2[:, 1:2], EPS, None, ALU.add)
                dve.drain()

            def stds(n):
                dve.nop().then_inc(var_ready, 1)
                dve.wait_ge(std_ready, n)
                V.reciprocal(rstd[:, :], rstd[:, :])
                dve.drain()

            def normalised(dst, src, t):
                V.tensor_scalar(dst, src, mean[:, bass.ds(t, 1)], rstd[:, bass.ds(t, 1)], ALU.subtract, ALU.mult)
                dve.drain()

            def rectified_parts(t, h):
                V.tensor_scalar(h, h, 0.0, None, ALU.max)
                dve.drain()
                V.tensor_copy(tile4(parts, t, 0), h)
                dve.drain()
                V.tensor_tensor(tile4(parts, t, 1), h, tile4(parts, t, 0), ALU.subtract)
                dve.drain()

            tiles_loop(dve, lambda t, m, b: norm_stats(tile3(xcur, t), t))
            stds(1)

            def first_norm(t, m, b):
                normalised(ht[0][:, :], tile3(xcur, t), t)
                rectified_parts(t, ht[0][:, :])
            tiles_loop(dve, first_norm)
            dve.nop().then_inc(h_ready, 1)
            dve.wait_ge(consts_ready, 1)
            dve.wait_ge(weights_in, DMA * 7)

            def convolve(t, m, b):
                dve.wait_ge(s_stored[b], DMA * (m + 1))
                for g, (k0, n) in enumerate(ADJ_GROUPS):
                    if g % 2 == 0:
                        dve.wait_ge(adj_flipped, t * NA + g + 9)
                        V.tensor_copy(flat(s_tile[b][:, k0:k0 + n, :]), flip_ps[0][:, :].bitcast(BF16)[:, 0:n * P]).then_inc(adj_moved_v, 1)
                dve.wait_ge(conv_done, t + 1)
                V.tensor_tensor(tile3(s_tile[b], t), tile3(s_tile[b], t), ident_bf[:, :], ALU.add).then_inc(s_made, 1)
                dve.wait_ge(proj_done, t + 1)
                V.scalar_tensor_tensor(out=tile3(x1_all, t), in0=b0_sb[:, :], scalar=row_n[:, bass.ds(t, 1)],
                                            in1=pv_ps[:, D:2 * D], op0=ALU.mult, op1=ALU.add).then_inc(proj_out, 1)
            tiles_loop(dve, convolve)

            dve.wait_ge(cols_done, 1)
            V.tensor_copy(col_n[:, :], lg[0][:, 0:NT])
            dve.drain()
            V.tensor_copy(deg_inv[:, :], col_n[:, :])
            dve.drain()
            V.tensor_tensor(deg_inv[:, NT - 1:NT], deg_inv[:, NT - 1:NT], ident[:, P - 1:P], ALU.add)
            dve.drain()
            V.reciprocal(deg_inv[:, :], deg_inv[:, :])
            for sums, inverse in ((row_n, row_inv), (col_n, col_inv)):
                V.tensor_scalar(inverse[:, :], sums[:, :], 1.0, 1e-12, ALU.add, ALU.max)
                dve.drain()
                V.reciprocal(inverse[:, :], inverse[:, :])
            dve.drain()

            V.tensor_scalar(real_row[:, :], ident[:, P - 1:P], -1.0, 1.0, ALU.mult, ALU.add)
            dve.drain()

            def second_stats(t, m, b):
                V.scalar_tensor_tensor(out=tile3(x1_all, t), in0=tile3(x1_all, t), scalar=deg_inv[:, bass.ds(t, 1)],
                                       in1=tile3(xcur, t), op0=ALU.mult, op1=ALU.add)
                dve.drain()
                norm_stats(tile3(x1_all, t), t)
            tiles_loop(dve, second_stats)
            dve.nop().then_inc(x1_ready, 1)
            stds(2)

            def second_norm(t, m, b):
                dve.wait_ge(first_turned, t + 1)
                normalised(ht[b][:, :], tile3(x1_all, t), t)
                rectified_parts(t, ht[b][:, :])
                V.tensor_copy(tile3(xcur, t), ht[b][:, :]).then_inc(tile_ready, 1)
            tiles_loop(dve, second_norm)
            dve.drain()
            dve.nop().then_inc(second_ready, 1)

            for s in range(2):
                def copy_logits(t, b):
                    if not (isinstance(t, int) and t == 0):
                        dve.wait_ge(p_flipped[s], (t - 1) * NG + 1)
                    for c, (c0, w) in enumerate(LOGIT_CHUNKS):
                        w = min(w, N - c0)
                        dve.wait_ge(logits_ready[s], t * NL + c + 1)
                        V.tensor_scalar(expo[b][:, c0:c0 + w], lg[c % 2][:, 0:w], 1.0, None, ALU.mult, ALU.max,
                                             accum_out=maxes[:, c:c + 1]).then_inc(logits_used[s], 1)
                    dve.drain()
                    V.tensor_reduce(out=top[:, :], in_=maxes[:, :], axis=AX.X, op=ALU.max)
                    dve.drain()
                    V.tensor_scalar(neg_max[b][:, :], top[:, :], -1.0, None, ALU.mult).then_inc(logits_copied[s], 1)

                def bisect(b, r):
                    V.scalar_tensor_tensor(out=window[:, 0:N], in0=expo[b][:, 0:N], scalar=cut[b][:, :].bitcast(FP32),
                                           in1=expo[b][:, 0:N], op0=ALU.is_ge, op1=ALU.mult, accum_out=mass[:, :])
                    dve.drain()
                    if r < ROUNDS[s] - 1:
                        V.tensor_scalar(move[:, :], mass[:, :], target[b][:, :], 0.5, ALU.is_ge, ALU.subtract)
                        scale = width[b][:, r + 1:r + 2]
                    else:
                        V.tensor_scalar(move[:, :], mass[:, :], target[b][:, :], None, ALU.is_ge)
                        scale = width[b][:, r + 1:r + 2]
                    dve.drain()
                    V.scalar_tensor_tensor(out=cut[b][:, :], in0=move[:, :], scalar=scale, in1=cut[b][:, :], op0=ALU.mult,
                                           op1=ALU.add)
                    dve.drain()

                def find_odd(flags, t):
                    if is_last(t):
                        V.tensor_tensor(flags, flags, real_row[:, :], ALU.mult)
                        dve.drain()
                    V.tensor_copy(odd[:, 0:1], flags)
                    dve.drain()
                    V.transpose(odd_t[:, :], odd[:, :])
                    dve.drain()
                    V.tensor_reduce(out=odd_q[:, :], in_=odd_t[:, :], axis=AX.X, op=ALU.max)
                    dve.drain()
                    for q in range(4):
                        V.tensor_copy(odd4[0:1, q:q + 1], odd_q[32 * q:32 * q + 1, :])
                    dve.drain()
                    V.tensor_reduce(out=odd_n[:, :], in_=odd4[:, :], axis=AX.X, op=ALU.max)
                    dve.drain()

                def keep_flags(b):
                    V.tensor_tensor_scan(csum[:, 1:9], ones8[:, :], top8[:, :], mass[:, :], ALU.mult, ALU.add)
                    V.tensor_copy(csum[:, 0:1], mass[:, :])
                    dve.drain()
                    V.tensor_scalar(keep8[:, :], csum[:, 0:8], target[b][:, :], None, ALU.is_lt)
                    dve.drain()

                def step(t, m, b):
                    dve.wait_ge(expo_ready[s], t + 1)
                    for r in range(ROUNDS_SCALAR[s], ROUNDS[s]):
                        if r == ROUNDS_SCALAR[s] + ROUNDS_BEFORE_NEXT[s] and not is_last(t):
                            copy_logits(t + 1, 1 - b)
                        bisect(b, r)
                    V.scalar_tensor_tensor(out=window[:, 0:N], in0=expo[b][:, 0:N], scalar=cut[b][:, :].bitcast(FP32),
                                           in1=expo[b][:, 0:N], op0=ALU.is_lt, op1=ALU.mult, accum_out=mass[:, :])
                    dve.drain()
                    V.max(out=top8[:, :], in_=window[:, 0:N])
                    V.scalar_tensor_tensor(out=mass[:, :], in0=mass[:, :], scalar=-1.0, in1=total[b][:, :], op0=ALU.mult,
                                           op1=ALU.add)
                    dve.drain()
                    keep_flags(b)
                    V.tensor_tensor(edge[:, :], keep8[:, 0:7], keep8[:, 1:8], ALU.subtract)
                    dve.drain()
                    V.scalar_tensor_tensor(out=pick[:, 0:7], in0=edge[:, :], scalar=1.0, in1=top8[:, 0:7], op0=ALU.mult,
                                           op1=ALU.mult, accum_out=least[:, :])
                    dve.drain()
                    V.scalar_tensor_tensor(out=pick[:, 0:7], in0=edge[:, :], scalar=1.0, in1=top8[:, 1:8], op0=ALU.mult,
                                           op1=ALU.mult, accum_out=below[:, :])
                    dve.drain()
                    V.tensor_tensor(pick[:, 0:1], least[:, :], below[:, :], ALU.is_le)
                    dve.drain()
                    find_odd(pick[:, 0:1], t)
                    left = dve.alloc_register(nc.get_next_instruction_name() + "_left")
                    dve.reg_load(left, odd_n[0:1, 0:1])
                    with dve.If(dve.snap(left) < 1):
                        V.scalar_tensor_tensor(out=expo[b][:, 0:N], in0=expo[b][:, 0:N], scalar=least[:, :],
                                               in1=expo[b][:, 0:N], op0=ALU.is_ge, op1=ALU.mult, accum_out=kept[:, :])
                        dve.drain()
                    with dve.Else():
                        with dve.While(left):
                            V.tensor_tensor(pick[:, :], top8[:, :], keep8[:, :], ALU.mult)
                            dve.drain()
                            V.tensor_reduce(out=least[:, :], in_=pick[:, :], axis=AX.X, op=ALU.add)
                            dve.drain()
                            V.scalar_tensor_tensor(out=pick[:, :], in0=keep8[:, :], scalar=-1.0, in1=pick[:, :],
                                                   op0=ALU.add, op1=ALU.add)
                            V.tensor_tensor(mass[:, :], mass[:, :], least[:, :], ALU.add)
                            dve.drain()
                            V.match_replace(out=window[:, :], in_to_replace=pick[:, :], in_values=window[:, :],
                                            imm_value=-1.0)
                            dve.drain()
                            V.max(out=top8[:, :], in_=window[:, 0:N])
                            V.tensor_tensor(below[:, :], mass[:, :], target[b][:, :], ALU.is_lt)
                            dve.drain()
                            keep_flags(b)
                            find_odd(below[:, :], t)
                            dve.reg_load(left, odd_n[0:1, 0:1])
                        V.scalar_tensor_tensor(out=expo[b][:, 0:N], in0=window[:, 0:N], scalar=0.0, in1=expo[b][:, 0:N],
                                               op0=ALU.max, op1=ALU.subtract, accum_out=kept[:, :])
                        dve.drain()
                    dve.end_ifs()
                    dve.wait_ge(xa_ready[s], t + 1)
                    V.reciprocal(kept_inv[b][:, :], kept[:, :]).then_inc(probs_ready[s], 1)
                    dve.drain()

                if s == 1:
                    dve.wait_ge(p_flipped[0], NT * NG + 1)
                for b in range(2):
                    V.memset(expo[b][:, N:NP], 0.0)
                dve.drain()
                copy_logits(0, 0)
                tiles_loop(dve, step)

            dve.wait_ge(y_out[1], NT + 1)
            tiles_loop(dve, lambda t, m, b: norm_stats(tile3(y_all, t), t))
            stds(3)
            dve.wait_ge(x1_in, DMA * 3)

            def last_norm(t, m, b):
                normalised(ht[b][:, :], tile3(y_all, t), t)
                V.tensor_tensor(ht[b][:, :], ht[b][:, :], gamma_sb, ALU.mult)
                dve.drain()
                V.tensor_tensor(ht[b][:, :], ht[b][:, :], beta_sb, ALU.add)
                dve.drain()
                V.tensor_tensor(tile3(xcur, t), tile3(xcur, t), ht[b][:, :], ALU.add)
                dve.drain()
            tiles_loop(dve, last_norm)
            dve.nop().then_inc(y_norm, 1)


_INS = ["x", "adj", "L0_gnn_W", "L0_gnn_b", "L1_gnn_W1", "L1_gnn_W2", "L1_gnn_W3", "L1_gnn_U1", "L1_gnn_U2",
        "L1_gnn_U3", "L1_gnn_gamma", "L1_gnn_beta"]


def kernel(**inputs):
    import numpy as np
    import concourse.bacc as bacc
    from concourse.bass_utils import run_bass_kernel_spmd

    nc = bacc.Bacc("TRN2", target_bir_lowering=False, num_devices=1)
    arrays, args = {}, []
    for name in _INS:
        a = np.ascontiguousarray(inputs[name])
        arrays[f"in_{name}"] = a
        args.append(nc.dram_tensor(f"in_{name}", a.shape, mybir.dt.from_np(a.dtype), kind="ExternalInput").ap())
    args.append(nc.dram_tensor("result", (N, D), FP32, kind="ExternalOutput").ap())
    graph_layers(nc, *args)
    r = run_bass_kernel_spmd(nc, [arrays], core_ids=[0])
    return r.results[0]["result"]
```

```python
import concourse.bass as bass
from concourse import mybir
from contextlib import ExitStack

FP32 = mybir.dt.float32
BF16 = mybir.dt.bfloat16
FP16 = mybir.dt.float16
I32 = mybir.dt.int32
ALU = mybir.AluOpType
ACT = mybir.ActivationFunctionType
AX = mybir.AxisListType

P = 128
N = 3327
D = 256
DA = 64
DC = D // P
NT = (N + P - 1) // P
NP = NT * P
TAIL = N - (NT - 1) * P
EPS = 1e-5
NUCLEUS = 0.9
DMA = 16

TOP = (127 << 23) + 128
LEAST_SHARE = 0.09 / N
GRAIN = 1 << 20
ROUNDS = (8, 11)
ROUNDS_SCALAR = (3, 4)
ROUNDS_BEFORE_NEXT = ((0, 1), (0, 1))
WIDTHS = max(ROUNDS) + 1

HALVES = ((0, NT // 2), (NT // 2, NT))
CHUNK = 1024
LOGIT_CHUNKS = [(c, min(CHUNK, NP - c)) for c in range(0, NP, CHUNK)]
NL = len(LOGIT_CHUNKS)
LOGITS_EARLY = list(range(min(2, NL)))
LOGITS_LATE = list(range(min(2, NL), NL))
FLIP_ADJ = 8
ADJ_GROUPS = [(k, min(FLIP_ADJ, NT - k)) for k in range(0, NT, FLIP_ADJ)]
NA = len(ADJ_GROUPS)
FLIP_P = 4
P_GROUPS = [(k, min(FLIP_P, NT - k)) for k in range(0, NT, FLIP_P)]
NG = len(P_GROUPS)


def graph_layers(nc, x, adj, w0, b0, w1, w2, w3, u1, u2, u3, gamma, beta, out):
    ctx = ExitStack()
    with ctx:
        def sb(name, shape, dt=FP32):
            return ctx.enter_context(nc.sbuf_tensor(name, shape, dt))

        def sem(name):
            return ctx.enter_context(nc.semaphore(name))

        s_dram = nc.dram_tensor("s_scratch", [NT, P, NP], BF16, kind="Internal").ap()
        x1_dram = nc.dram_tensor("x1_scratch", [P, NT * D], FP32, kind="Internal").ap()
        xa_dram = nc.dram_tensor("xa_scratch", [NT, P, D], FP32, kind="Internal").ap()
        q_dram = nc.dram_tensor("q_scratch", [2, NT, DA, P], FP32, kind="Internal").ap()
        y_dram = nc.dram_tensor("y_scratch", [NT, P, D], FP32, kind="Internal").ap()

        xcur = sb("xcur", [P, NT, D])
        parts = sb("parts", [P, NT, 2, D], FP16)
        both = sb("both", [P, NT, 2, 2 * D], FP16)
        k_t = sb("k_t", [P, NP])
        y_all = parts[:, :, :, :].rearrange("p t a d -> p (t a d)").bitcast(FP32).rearrange("p (t d) -> p t d", t=NT)
        x1_all = both[:, 0:NT // 2, :, :].rearrange("p t a d -> p (t a d)").bitcast(FP32).rearrange(
            "p (t d) -> p t d", t=NT)
        expo = [sb(f"expo{b}", [P, NP]) for b in range(2)]
        natural = [expo[b][:, 0:NP // 2].bitcast(BF16) for b in range(2)]
        window = sb("window", [P, NP + 8])
        terms = sb("terms", [P, N], mybir.dt.uint8)
        probs_t = sb("probs_t", [P, NP])
        q_stage = sb("q_stage", [P, P])
        ident_bf = q_stage[:, 0:P // 2].bitcast(BF16)
        zeros_bf = q_stage[:, P // 2:P].bitcast(BF16)
        s_tile = [sb(f"s_tile{b}", [P, NT, P], BF16) for b in range(2)]
        q_tile = [sb(f"q_tile{b}", [P, P]) for b in range(2)]
        ht = [sb(f"ht{b}", [P, D]) for b in range(2)]
        xfb = sb("xfb", [P, 2 * D])
        turned = sb("turned", [P, (3 * DC + 1) * P])
        xfbt = turned[:, 0:2 * DC * P].rearrange("p (c i) -> p c i", c=2 * DC)
        xt = turned[:, 2 * DC * P:3 * DC * P].rearrange("p (c i) -> p c i", c=DC)
        unused = turned[:, :].bitcast(mybir.dt.uint8)[:, 0:N]
        y_tile = sb("y_tile", [P, D])
        y_in = y_tile
        qraw = sb("qraw", [DA, P])
        w0_sb = probs_t[:, 0:DC * D].rearrange("p (c n) -> p c n", c=DC)
        b0_sb = probs_t[:, DC * D:(DC + 1) * D]
        w1_sb = sb("w1_sb", [P, DC, DA])
        w3_sb = sb("w3_sb", [P, DC, 2, DA])
        w2_sb = sb("w2_sb", [DA, 2, DA])
        u_sb = sb("u_sb", [P, 3, DC, D])
        gamma_sb = u_sb[:, 0, 0, :]
        beta_sb = u_sb[:, 0, 1, :]
        ident = sb("ident", [P, P])
        ones_bf = sb("ones_bf", [P, 1], BF16)
        ones8 = sb("ones8", [P, 8])
        stats = sb("stats", [P, NT, 6])
        mean = sb("mean", [P, NT])
        var = sb("var", [P, NT])
        rstd = sb("rstd", [P, NT])
        row_n = sb("row_n", [P, NT])
        col_n = sb("col_n", [P, NT])
        deg_inv = sb("deg_inv", [P, NT])
        row_inv = sb("row_inv", [P, NT])
        col_inv = sb("col_inv", [P, NT])
        maxes = sb("maxes", [P, NL])
        neg_max = [sb(f"neg_max{b}", [P, 1]) for b in range(2)]
        total = [sb(f"total{b}", [P, 1]) for b in range(2)]
        kept_inv = [sb(f"kept_inv{b}", [P, 1]) for b in range(2)]
        target = [sb(f"target{b}", [P, 1]) for b in range(2)]
        slack = sb("slack", [P, 1])
        width = [sb(f"width{b}", [P, WIDTHS]) for b in range(2)]
        halves = sb("halves", [P, WIDTHS])
        signs = sb("signs", [P, 1])
        lack = sb("lack", [P, 1])
        low = sb("low", [P, 1])
        span_n = sb("span_n", [P, 1], I32)
        span = sb("span", [P, 1])
        neg_count = sb("neg_count", [P, 1])
        side = sb("side", [P, 1])
        mass = sb("mass", [P, 1])
        move = sb("move", [P, 1])
        cut = [sb(f"cut{b}", [P, 1], I32) for b in range(2)]
        top8 = sb("top8", [P, 8])
        csum = sb("csum", [P, 9])
        keep8 = sb("keep8", [P, 8])
        edge = sb("edge", [P, 7])
        pick = sb("pick", [P, 8])
        least = sb("least", [P, 1])
        real_row = sb("real_row", [P, 1])
        top = sb("top", [P, 1])
        kept = sb("kept", [P, 1])
        below = sb("below", [P, 1])
        odd = sb("odd", [P, 32])
        odd_t = sb("odd_t", [P, 32])
        odd_q = sb("odd_q", [P, 1])
        odd4 = sb("odd4", [1, 4])
        odd_n = sb("odd_n", [1, 1], I32)

        bank = [ctx.enter_context(nc.psum_tensor(f"bank{i}", [P, 512], FP32)) for i in range(4)]
        lg = [ctx.enter_context(nc.psum_tensor(f"lg{i}", [P, CHUNK], FP32)) for i in range(2)]
        flip_ps = bank[0:2]
        pv_ps = bank[2]
        s_ps = bank[3]

        x_in = sem("x_in")
        weights_in = sem("weights_in")
        x1_stored = sem("x1_stored")
        xa_in = sem("xa_in")
        x1_in = sem("x1_in")
        out_done = sem("out_done")
        x_pad = sem("x_pad")
        consts_ready = sem("consts_ready")
        var_ready = sem("var_ready")
        std_ready = sem("std_ready")
        h_ready = sem("h_ready")
        h_made = sem("h_made")
        high_made = sem("high_made")
        cols_done = sem("cols_done")
        x1_ready = sem("x1_ready")
        second_ready = sem("second_ready")
        y_norm = sem("y_norm")
        conv_done = sem("conv_done")
        conv_turned = sem("conv_turned")
        conv_turned_out = sem("conv_turned_out")
        proj_done = sem("proj_done")
        s_made = sem("s_made")
        tile_ready = sem("tile_ready")
        first_x = sem("first_x")
        first_qk_step = sem("first_qk_step")
        nat_in = [sem(f"nat_in_{n}") for n in range(2)]
        s_stored = [sem(f"s_stored_{n}") for n in range(2)]
        adj_flipped = sem("adj_flipped")
        adj_moved_v = sem("adj_moved_v")
        adj_moved_s = sem("adj_moved_s")
        conv_out = sem("conv_out")
        proj_out = sem("proj_out")
        first_turned = sem("first_turned")
        first_qk_out = sem("first_qk_out")
        logits_ready = [sem(f"logits_ready_{n}") for n in range(2)]
        logits_copied = [sem(f"logits_copied_{n}") for n in range(2)]
        expo_ready = [sem(f"expo_ready_{n}") for n in range(2)]
        probs_ready = [sem(f"probs_ready_{n}") for n in range(2)]
        p_moved = [sem(f"p_moved_{n}") for n in range(2)]
        pv_done = [sem(f"pv_done_{n}") for n in range(2)]
        x_turned = [sem(f"x_turned_{n}") for n in range(2)]
        x_t_ready = [sem(f"x_t_ready_{n}") for n in range(2)]
        qk_step = [sem(f"qk_step_{n}") for n in range(2)]
        u_in = [sem(f"u_in_{n}") for n in range(2)]
        s_in = [[sem(f"s_in_{n}_{b}") for b in range(2)] for n in range(2)]
        q_in = [[sem(f"q_in_{n}_{b}") for b in range(2)] for n in range(2)]
        xa_stored = [[sem(f"xa_stored_{n}_{b}") for b in range(2)] for n in range(2)]
        y_stored = [sem(f"y_stored_{n}") for n in range(2)]
        y_loaded = [sem(f"y_loaded_{n}") for n in range(2)]
        q_stored = [sem(f"q_stored_{n}") for n in range(2)]
        s_done = [sem(f"s_done_{n}") for n in range(2)]
        fb_ready = [sem(f"fb_ready_{n}") for n in range(2)]
        fb_turned = [sem(f"fb_turned_{n}") for n in range(2)]
        lo_ready = [sem(f"lo_ready_{n}") for n in range(2)]
        logits_used = [sem(f"logits_used_{n}") for n in range(2)]
        p_flipped = [sem(f"p_flipped_{n}") for n in range(2)]
        xa_ready = [sem(f"xa_ready_{n}") for n in range(2)]
        y_out = [sem(f"y_out_{n}") for n in range(2)]
        y_done = [sem(f"y_done_{n}") for n in range(2)]
        qk_out = [sem(f"qk_out_{n}") for n in range(2)]
        free_slots = [
            *[(s_stored[n], DMA) for n in range(2)],
            (adj_flipped, 8),
            (adj_moved_v, 1),
            (adj_moved_s, 1),
            (conv_out, 1),
            (proj_out, 1),
            (first_turned, 2),
            (first_qk_out, 2),
            *[(xa_stored[n][b], DMA) for n in range(2) for b in range(2)],
            *[(y_stored[n], DMA) for n in range(2)],
            *[(q_stored[n], DMA) for n in range(2)],
            *[(s_done[n], 2) for n in range(2)],
            *[(fb_ready[n], 1) for n in range(2)],
            *[(fb_turned[n], 1) for n in range(2)],
            *[(lo_ready[n], 1) for n in range(2)],
            *[(logits_used[n], 2) for n in range(2)],
            *[(p_flipped[n], 1) for n in range(2)],
            *[(xa_ready[n], 2) for n in range(2)],
            *[(y_out[n], 1) for n in range(2)],
            *[(y_done[n], 1) for n in range(2)],
            *[(qk_out[n], 2) for n in range(2)],
        ]

        V, A, G, T = nc.vector, nc.scalar, nc.gpsimd, nc.tensor

        def tiles_loop(eng, body):
            with eng.Fori(0, NT // 2 - 1) as i:
                for b in range(2):
                    body(i * 2 + b, i, b)
            for b in range(2):
                body(NT - 2 + b, NT // 2 - 1, b)

        def is_last(t):
            return isinstance(t, int) and t == NT - 1

        def tile3(buf, t):
            return buf[:, t, :] if isinstance(t, int) else buf[:, bass.ds(t, 1), :].rearrange("p a d -> p (a d)")

        def tile4(buf, t, part):
            if isinstance(t, int):
                return buf[:, t, part, :]
            return buf[:, bass.ds(t, 1), part:part + 1, :].rearrange("p a q d -> p (a q d)")

        def dram_tile(buf, t):
            return buf[t] if isinstance(t, int) else buf[bass.ds(t, 1)].rearrange("a p n -> (a p) n")

        def flat(ap):
            return ap.rearrange("p a b -> p (a b)")

        block = ctx.enter_context(nc.Block())

        @block.sync
        def _(sp):
            def spread(v):
                return v.rearrange("(a n) -> a n", a=1).broadcast_to([P, D])

            sp.wait_ge(x_pad, 1)
            sp.dma_start(xcur[:, 0:NT - 1, :], x[0:(NT - 1) * P, :].rearrange("(t p) d -> p t d", p=P)).then_inc(x_in, DMA)
            sp.dma_start(xcur[0:TAIL, NT - 1, :], x[(NT - 1) * P:N, :]).then_inc(x_in, DMA)
            sp.dma_start(w0_sb[:, :, :], w0.rearrange("(c p) n -> p c n", p=P)).then_inc(weights_in, DMA)
            sp.dma_start(b0_sb[:, :], spread(b0)).then_inc(weights_in, DMA)
            sp.dma_start(w1_sb[:, :, :], w1.rearrange("(c p) n -> p c n", p=P)).then_inc(weights_in, DMA)
            for j in range(2):
                sp.dma_start(w3_sb[:, :, j, :], w3.rearrange("(c p) n -> p c n", p=P)).then_inc(weights_in, DMA)
                sp.dma_start(w2_sb[:, j, :], w2).then_inc(weights_in, DMA)

            def load_u(s):
                for j, u in enumerate((u1, u2, u3)):
                    sp.dma_start(u_sb[:, j, :, :], u[s].rearrange("(c p) n -> p c n", p=P)).then_inc(u_in[s], DMA)
            load_u(0)

            def store_s(t, m, b):
                sp.wait_ge(s_made, t + 1)
                sp.dma_start(dram_tile(s_dram, t), flat(s_tile[b][:, :, :])).then_inc(s_stored[b], DMA)
            tiles_loop(sp, store_s)
            sp.wait_ge(x1_ready, 1)
            sp.dma_start(x1_dram, flat(x1_all)).then_inc(x1_stored, DMA)
            for b in range(2):
                sp.wait_ge(s_stored[b], DMA * (NT // 2 + 1))

            for s in range(2):
                def load_q(t, b):
                    sp.dma_start(q_tile[b][DA * s:DA * (s + 1), :], dram_tile(q_dram[s], t)).then_inc(q_in[s][b], DMA)
                sp.wait_ge(q_stored[s], DMA * (NT + 1))
                for t in range(2):
                    load_q(t, t)

                def load(t, m, b):
                    if not (isinstance(t, int) and t >= NT - 2):
                        sp.wait_ge(logits_ready[s], (t + 1) * NL)
                        load_q(t + 2, b)
                    sp.wait_ge(s_done[s], t + 1)
                    sp.dma_start(flat(s_tile[b][:, :, :]), dram_tile(s_dram, t)).then_inc(s_in[s][b], DMA)
                    if s == 1:
                        sp.wait_ge(y_done[1], t + 1)
                        sp.dma_start(y_in[:, :], dram_tile(y_dram, t)).then_inc(y_loaded[1], DMA)
                tiles_loop(sp, load)
                if s == 0:
                    for b in range(2):
                        sp.wait_ge(xa_stored[0][b], DMA * (NT // 2 + 1))
                    sp.wait_ge(y_stored[0], DMA * (NT + 1))
                    sp.wait_ge(y_done[0], NT + 1)
                    sp.dma_start(xcur[:, :, :], xa_dram.rearrange("t p d -> p t d")).then_inc(xa_in, DMA)
                    load_u(1)
            sp.wait_ge(y_done[1], NT + 1)
            sp.dma_start(flat(xcur[:, :, :]), x1_dram).then_inc(x1_in, DMA)
            sp.dma_start(gamma_sb, spread(gamma)).then_inc(x1_in, DMA)
            sp.dma_start(beta_sb, spread(beta)).then_inc(x1_in, DMA)
            for half, (t0, t1) in enumerate(((HALVES[0]), (HALVES[1][0], NT - 1))):
                sp.wait_ge(y_norm, half + 1)
                sp.dma_start(out[t0 * P:t1 * P, :].rearrange("(t p) d -> p t d", p=P), xcur[:, t0:t1, :]).then_inc(out_done, DMA)
            sp.dma_start(out[(NT - 1) * P:N, :], xcur[0:TAIL, NT - 1, :]).then_inc(out_done, DMA)
            sp.wait_ge(out_done, DMA * 3)

        @block.gpsimd
        def _(pool):
            for m in (ident, ident_bf):
                G.memset(m[:, :], 0.0)
            pool.drain()
            for m in (ident, ident_bf):
                G.affine_select(out=m[:, :], in_=m[:, :], compare_op=ALU.not_equal, fill=1.0, base=0,
                                pattern=[[-1, P]], channel_multiplier=1)
            G.memset(ones_bf[:, :], 1.0)
            G.memset(zeros_bf[:, :], 0.0)
            G.memset(ones8[:, :], 1.0)
            G.memset(odd[:, :], 0.0)
            for r in range(WIDTHS):
                G.memset(halves[:, r:r + 1], 0.5 ** r)
            for b in range(2):
                G.memset(natural[b][:, N:NP], 0.0)
            G.memset(window[:, N:NP], 0.0)
            G.memset(window[:, NP:NP + 8], -1.0)
            pool.drain()
            pool.nop().then_inc(consts_ready, 1)

            def load_adj(t, m, b):
                pool.wait_ge(adj_flipped, (t - 1) * NA + 8)
                pool.wait_ge(x_in, DMA * 2)
                if is_last(t):
                    G.memset(natural[b][:, :], 0.0)
                    pool.drain()
                    pool.dma_start(natural[b][0:TAIL, 0:N], adj[(NT - 1) * P:N, :]).then_inc(nat_in[b], DMA)
                else:
                    pool.dma_start(natural[b][:, 0:N], adj[bass.ds(t * P, P), :]).then_inc(nat_in[b], DMA)
            tiles_loop(pool, load_adj)

            pool.wait_ge(x1_stored, DMA)
            def low_parts(t, m, b):
                pool.wait_ge(fb_ready[0], t + 2)
                G.tensor_tensor(tile4(both, t, 1), xfb[:, :], tile4(both, t, 0), ALU.subtract).then_inc(lo_ready[0], 1)
            tiles_loop(pool, low_parts)

        @block.scalar
        def _(act):
            act.wait_ge(var_ready, 1)
            A.activation(rstd[:, :], var[:, :], ACT.Sqrt).then_inc(std_ready, 1)

            for half, (t0, t1) in enumerate(HALVES):
                act.wait_ge(h_made, half + 1)
                A.activation(parts[:, t0:t1, 0, :], x1_all[:, t0:t1, :], ACT.Copy).then_inc(high_made, 1)

            def convolve(t, m, b):
                act.wait_ge(s_stored[b], DMA * (m + 1))
                for g, (k0, n) in enumerate(ADJ_GROUPS):
                    if g % 2:
                        act.wait_ge(adj_flipped, t * NA + g + 9)
                        A.activation(flat(s_tile[b][:, k0:k0 + n, :]), flip_ps[1][:, :].bitcast(BF16)[:, 0:n * P],
                                          ACT.Copy).then_inc(adj_moved_s, 1)
                act.wait_ge(conv_done, t + 1)
                A.activation(y_tile[:, :], s_ps[:, 0:D], ACT.Copy)
                A.activation(row_n[:, bass.ds(t, 1)], s_ps[:, D:D + 1], ACT.Copy).then_inc(conv_out, 1)
                act.wait_ge(conv_turned, t + 1)
                A.activation(flat(xt[:, :, :]), pv_ps[:, 0:D], ACT.Copy).then_inc(conv_turned_out, 1)
            tiles_loop(act, convolve)
            act.wait_ge(var_ready, 2)
            A.activation(rstd[:, :], var[:, :], ACT.Sqrt).then_inc(std_ready, 1)

            def query_key(t, half, steps, outs):
                raw_query_key(t, half, steps, outs)
                second_query(t, half, steps, outs)

            def raw_query_key(t, half, steps, outs):
                r0, r1 = DA * half, DA * (half + 1)
                act.wait_ge(steps, t * 2 + 1)
                A.activation(qraw[:, :], flip_ps[0][0:DA, 0:P], ACT.Copy)
                A.activation(k_t[r0:r1, bass.ds(t * P, P)], flip_ps[0][r0:r1, P:2 * P], ACT.Copy).then_inc(outs, 1)

            def second_query(t, half, steps, outs):
                r0, r1 = DA * half, DA * (half + 1)
                act.wait_ge(steps, t * 2 + 2)
                act.wait_ge(q_stored[half], DMA * (t + 1))
                A.activation(q_stage[r0:r1, :], flip_ps[0][r0:r1, 2 * P:3 * P], ACT.Copy).then_inc(outs, 1)
                act.wait_ge(outs, t * 2 + 4)
                act.dma_start(dram_tile(q_dram[half], t), q_stage[r0:r1, :]).then_inc(q_stored[half], DMA)

            def first_query_key(t, m, b):
                act.wait_ge(first_turned, t + 3)
                A.activation(flat(xt[:, :, :]), pv_ps[:, D:2 * D], ACT.Copy).then_inc(first_x, 1)
                query_key(t, 0, first_qk_step, first_qk_out)
            tiles_loop(act, first_query_key)
            act.wait_ge(second_ready, 1)
            act.wait_ge(x1_stored, DMA)

            for s in range(2):
                act.drain()
                r0, r1 = DA * s, DA * (s + 1)

                def exponentials(t, b):
                    act.wait_ge(logits_copied[s], t + 1)
                    A.activation(expo[b][:, 0:N], expo[b][:, 0:N], ACT.Exp, bias=neg_max[b][:, :],
                                 accum_out=total[b][:, :])
                    act.drain()
                    A.activation(low[:, :], total[b][:, :], ACT.Copy, scale=LEAST_SHARE)
                    A.activation(slack[:, :], total[b][:, :], ACT.Copy, scale=1.0 - NUCLEUS)
                    A.activation(target[b][:, :], total[b][:, :], ACT.Copy, scale=NUCLEUS)
                    act.drain()
                    A.activation(span_n[:, :], low[:, :].bitcast(I32), ACT.Copy, scale=-1.0 / GRAIN,
                                 bias=float(TOP // GRAIN + 1))
                    act.drain()
                    A.activation(span[:, :], span_n[:, :], ACT.Copy, scale=float(GRAIN))
                    act.drain()
                    A.activation(width[b][:, :], halves[:, :], ACT.Copy, scale=span[:, :])
                    A.activation(cut[b][:, :], span[:, :], ACT.Copy, scale=-0.5, bias=float(TOP))
                    act.drain()

                def halve(b, r):
                    if r >= ROUNDS_SCALAR[s]:
                        return
                    A.activation(unused, expo[b][:, 0:N], ACT.Sign, scale=-1.0, bias=cut[b][:, :].bitcast(FP32),
                                 accum_out=signs[:, :])
                    act.drain()
                    A.activation(unused, expo[b][:, 0:N], ACT.Relu, scale=-1.0, bias=cut[b][:, :].bitcast(FP32),
                                 accum_out=lack[:, :])
                    A.activation(neg_count[:, :], signs[:, :], ACT.Copy, scale=-0.5, bias=-N / 2.0)
                    act.drain()
                    A.activation(side[:, :], neg_count[:, :], ACT.Identity, scale=cut[b][:, :].bitcast(FP32),
                                 bias=lack[:, :])
                    act.drain()
                    A.activation(side[:, :], side[:, :], ACT.Sign, bias=slack[:, :])
                    act.drain()
                    last = A.activation(cut[b][:, :], side[:, :], ACT.Identity, scale=width[b][:, r + 2:r + 3],
                                        bias=cut[b][:, :])
                    if r == ROUNDS_SCALAR[s] - 1:
                        last.then_inc(expo_ready[s], 1)
                    else:
                        act.drain()

                def diffused(t):
                    act.wait_ge(s_done[s], t + 3)
                    act.wait_ge(fb_turned[s], t + 1)
                    if s == 0:
                        act.wait_ge(lo_ready[0], t + 1)
                    A.activation(xfb[:, 0:D], s_ps[:, 0:D], ACT.Copy, scale=row_inv[:, bass.ds(t, 1)])
                    last = A.activation(xfb[:, D:2 * D], s_ps[:, 0:D] if s == 0 else s_ps[:, D:2 * D], ACT.Copy,
                                        scale=col_inv[:, bass.ds(t, 1)])
                    if s == 0:
                        act.drain()
                        last = A.activation(tile4(both, t, 0), xfb[:, :], ACT.Copy)
                    last.then_inc(fb_ready[s], 1)

                def step(t, m, b):
                    more = not (isinstance(t, int) and t >= NT - 2)
                    for g, (k0, n) in enumerate(P_GROUPS):
                        act.wait_ge(p_flipped[s], t * NG + g + 2)
                        A.activation(probs_t[:, k0 * P:(k0 + n) * P], flip_ps[g % 2][:, 0:n * P], ACT.Copy).then_inc(p_moved[s], 1)
                    if more:
                        exponentials(t + 2, b)
                        halve(b, 0)
                    act.wait_ge(pv_done[s], t + 1)
                    if s == 0:
                        act.wait_ge(xa_stored[0][b], DMA * (m + 1))
                    A.activation(ht[b][:, :], pv_ps[:, 0:D], ACT.Copy, scale=kept_inv[b][:, :]).then_inc(xa_ready[s], 1)
                    if more:
                        halve(b, 1)
                        act.drain()
                    act.wait_ge(fb_turned[s], t + 2)
                    if s == 0:
                        act.wait_ge(xa_ready[0], t + 3)
                        act.dma_start(dram_tile(xa_dram, t), ht[b][:, :]).then_inc(xa_stored[0][b], DMA)
                    act.wait_ge(x_turned[s], t + 1)
                    A.activation(flat(xfbt[:, :, :]), flip_ps[1][:, :], ACT.Copy)
                    A.activation(flat(xt[:, :, :]), pv_ps[:, D:2 * D], ACT.Copy).then_inc(x_t_ready[s], 1)
                    if s == 0:
                        query_key(t, 1, qk_step[0], qk_out[0])
                    if not is_last(t):
                        diffused(t + 1)
                    act.wait_ge(y_done[s], t + 2)
                    if s == 0:
                        act.wait_ge(y_stored[0], DMA * (t + 1))
                        A.activation(y_tile[:, :], pv_ps[:, 0:D], ACT.Copy).then_inc(y_out[0], 1)
                        act.wait_ge(y_out[0], t + 2)
                        act.dma_start(dram_tile(y_dram, t), y_tile[:, :]).then_inc(y_stored[0], DMA)
                    else:
                        A.activation(tile3(y_all, t), pv_ps[:, 0:D], ACT.Copy).then_inc(y_out[1], 1)
                    if more:
                        for r in range(2, ROUNDS_SCALAR[s]):
                            halve(b, r)
                for t in range(2):
                    exponentials(t, t)
                    for r in range(ROUNDS_SCALAR[s]):
                        halve(t, r)
                diffused(0)
                tiles_loop(act, step)
            act.wait_ge(var_ready, 3)
            A.activation(rstd[:, :], var[:, :], ACT.Sqrt).then_inc(std_ready, 1)

        @block.tensor
        def _(pe):
            pe.wait_ge(consts_ready, 1)
            pe.wait_ge(h_ready, 1)
            pe.wait_ge(weights_in, DMA * 7)
            T.matmul(lg[0][:, 0:NT], zeros_bf[:, :], zeros_bf[:, 0:NT], start=True, stop=True)

            def turn_convolved(t):
                pe.wait_ge(conv_out, t + 2)
                pe.wait_ge(proj_out, t + 1)
                for c in range(DC):
                    last = T.transpose(pv_ps[:, c * P:(c + 1) * P], y_tile[:, c * P:(c + 1) * P], ident[:, :])
                last.then_inc(conv_turned, 1)

            def project(t):
                pe.wait_ge(conv_turned_out, t + 1)
                for c in range(DC):
                    last = T.matmul(pv_ps[:, D:2 * D], xt[:, c, :], w0_sb[:, c, :], start=(c == 0), stop=(c == DC - 1))
                last.then_inc(proj_done, 1)

            def convolve(t, m, b, first=False):
                pe.wait_ge(nat_in[b], DMA * (m + 1))
                for k in range(NT):
                    T.matmul(lg[0][:, k:k + 1], natural[b][:, k * P:(k + 1) * P], ones_bf[:, :], start=False, stop=True,
                             skip_group_check=True)
                if not first:
                    turn_convolved(t - 1)
                for g, (k0, n) in enumerate(ADJ_GROUPS):
                    pe.wait_ge(adj_moved_s if g % 2 else adj_moved_v, t * (NA // 2) + g // 2 + 1)
                    view = flip_ps[g % 2][:, :].bitcast(BF16)
                    for k in range(n):
                        last = T.transpose(view[:, k * P:(k + 1) * P], natural[b][:, (k0 + k) * P:(k0 + k + 1) * P],
                                           ident_bf[:, :])
                    last.then_inc(adj_flipped, 1)
                    if g == 0 and not first:
                        project(t - 1)
                pe.wait_ge(adj_moved_v, (t + 1) * (NA // 2) + 1)
                pe.wait_ge(adj_moved_s, (t + 1) * (NA // 2) + 1)
                pe.wait_ge(conv_out, t + 1)
                for k in range(NT):
                    for part in range(2):
                        T.matmul(s_ps[:, 0:D], s_tile[b][:, k, :], parts[:, k, part, :], start=(k == 0 and part == 0),
                                 stop=(k == NT - 1 and part == 1), skip_group_check=True)
                    last = T.matmul(s_ps[:, D:D + 1], s_tile[b][:, k, :], ones_bf[:, :], start=False, stop=(k == NT - 1),
                                    skip_group_check=True)
                last.then_inc(conv_done, 1)

            convolve(0, 0, 0, first=True)
            with pe.Fori(0, NT // 2 - 1) as i:
                convolve(i * 2 + 1, i, 1)
                convolve(i * 2 + 2, i + 1, 0)
            convolve(NT - 1, NT // 2 - 1, 1)
            turn_convolved(NT - 1)
            project(NT - 1)
            T.matmul(lg[0][:, 0:NT], zeros_bf[:, :], zeros_bf[:, 0:NT], start=False, stop=True, skip_group_check=True).then_inc(cols_done, 1)

            def query_key(t, half, steps, outs):
                for c in range(DC):
                    T.matmul(flip_ps[0][0:DA, 0:P], w1_sb[:, c, :], xt[:, c, :], start=(c == 0), stop=(c == DC - 1))
                for c in range(DC):
                    last = T.matmul(flip_ps[0][:, P:2 * P], flat(w3_sb[:, c, :, :]), xt[:, c, :], start=(c == 0),
                                    stop=(c == DC - 1))
                last.then_inc(steps, 1)
                pe.wait_ge(outs, t * 2 + 3)
                T.matmul(flip_ps[0][:, 2 * P:3 * P], flat(w2_sb[:, :, :]), qraw[:, :], start=True, stop=True).then_inc(steps, 1)

            def first_query_key(t, m, b):
                pe.wait_ge(tile_ready, t + 1)
                pe.wait_ge(first_qk_out, t * 2 + 2)
                for c in range(DC):
                    last = T.transpose(pv_ps[:, D + c * P:D + (c + 1) * P], ht[b][:, c * P:(c + 1) * P], ident[:, :])
                last.then_inc(first_turned, 1)
                pe.wait_ge(first_x, t + 1)
                query_key(t, 0, first_qk_step, first_qk_out)
            tiles_loop(pe, first_query_key)
            pe.wait_ge(first_qk_out, 2 * NT + 2)
            pe.wait_ge(second_ready, 1)

            for s in range(2):
                r0, r1 = DA * s, DA * (s + 1)

                def logits(t, b, uses, chunks):
                    pe.wait_ge(q_in[s][b], DMA * uses)
                    for c in chunks:
                        c0, w = LOGIT_CHUNKS[c]
                        pe.wait_ge(logits_used[s], t * NL + c + 1)
                        for c1 in range(0, w, 512):
                            n = min(512, w - c1)
                            last = T.matmul(lg[c % 2][:, c1:c1 + n], q_tile[b][r0:r1, :], k_t[r0:r1, c0 + c1:c0 + c1 + n],
                                            start=True, stop=True)
                        last.then_inc(logits_ready[s], 1)

                def diffuse(t, b, uses):
                    pe.wait_ge(s_in[s][b], DMA * uses)
                    pe.wait_ge(fb_ready[s], t + 1)
                    width, src = (D, parts) if s == 0 else (2 * D, both)
                    for k in range(NT):
                        for part in range(2):
                            last = T.matmul(s_ps[:, 0:width], s_tile[b][:, k, :], src[:, k, part, :],
                                            start=(k == 0 and part == 0), stop=(k == NT - 1 and part == 1))
                    last.then_inc(s_done[s], 1)

                def step(t, m, b):
                    more = not (isinstance(t, int) and t >= NT - 2)
                    if more:
                        logits(t + 2, b, m + 2, LOGITS_EARLY)
                    pe.wait_ge(probs_ready[s], t + 1)
                    for g, (k0, n) in enumerate(P_GROUPS):
                        if g >= 2:
                            pe.wait_ge(p_moved[s], t * NG + g - 1)
                        for k in range(n):
                            last = T.transpose(flip_ps[g % 2][:, k * P:(k + 1) * P],
                                               window[:, (k0 + k) * P:(k0 + k + 1) * P], ident[:, :])
                        last.then_inc(p_flipped[s], 1)
                    if more:
                        logits(t + 2, b, m + 2, LOGITS_LATE)
                    pe.wait_ge(y_out[s], t + 1)
                    pe.wait_ge(p_moved[s], (t + 1) * NG)
                    for k in range(NT):
                        last = T.matmul(pv_ps[:, 0:D], probs_t[:, k * P:(k + 1) * P], xcur[:, k, :], start=(k == 0),
                                        stop=(k == NT - 1))
                    last.then_inc(pv_done[s], 1)
                    pe.wait_ge(fb_ready[s], t + 2)
                    for c in range(2 * DC):
                        last = T.transpose(flip_ps[1][:, c * P:(c + 1) * P], xfb[:, c * P:(c + 1) * P], ident[:, :])
                    last.then_inc(fb_turned[s], 1)
                    if not is_last(t):
                        diffuse(t + 1, 1 - b, m + 1 + b)
                    pe.wait_ge(xa_ready[s], t + 3)
                    for c in range(DC):
                        last = T.transpose(pv_ps[:, D + c * P:D + (c + 1) * P], ht[b][:, c * P:(c + 1) * P], ident[:, :])
                    last.then_inc(x_turned[s], 1)
                    pe.wait_ge(x_t_ready[s], t + 1)
                    if s == 0:
                        query_key(t, 1, qk_step[0], qk_out[0])
                    if s == 0:
                        T.matmul(pv_ps[:, 0:D], ident[:, :], tile3(xcur, t), start=True, stop=False)
                    else:
                        pe.wait_ge(y_loaded[1], DMA * (t + 1))
                        T.matmul(pv_ps[:, 0:D], ident[:, :], y_in[:, :], start=True, stop=False)
                    for j, turned_part in enumerate((xfbt[:, 0:DC, :], xfbt[:, DC:2 * DC, :], xt[:, :, :])):
                        for c in range(DC):
                            last = T.matmul(pv_ps[:, 0:D], turned_part[:, c, :], u_sb[:, j, c, :], start=False,
                                            stop=(j == 2 and c == DC - 1))
                    last.then_inc(y_done[s], 1)
                    if s == 0:
                        pe.wait_ge(qk_out[0], (t + 1) * 2 + 2)
                if s == 1:
                    pe.wait_ge(xa_in, DMA)
                    pe.wait_ge(lo_ready[0], NT + 1)
                pe.wait_ge(u_in[s], DMA * 3)
                for t in range(2):
                    logits(t, t, 1, LOGITS_EARLY + LOGITS_LATE)
                diffuse(0, 0, 1)
                tiles_loop(pe, step)

        @block.vector
        def _(dve):
            for slots, count in free_slots:
                dve.sem_inc(slots, count)
            V.memset(xcur[:, NT - 1, :], 0.0).then_inc(x_pad, 1)
            dve.wait_ge(x_in, DMA * 2)

            def norm_stats(src):
                dve.drain()
                tiles_loop(dve, lambda t, m, b: V.bn_stats(tile3(stats, t), tile3(src, t)))
                dve.drain()
                V.tensor_tensor(mean[:, :], stats[:, :, 1], stats[:, :, 4], ALU.add)
                V.tensor_tensor(rstd[:, :], stats[:, :, 1], stats[:, :, 4], ALU.subtract)
                V.tensor_tensor(var[:, :], stats[:, :, 2], stats[:, :, 5], ALU.add)
                dve.drain()
                V.tensor_scalar(mean[:, :], mean[:, :], 0.5, None, ALU.mult)
                V.tensor_tensor(rstd[:, :], rstd[:, :], rstd[:, :], ALU.mult)
                V.tensor_scalar(var[:, :], var[:, :], 1.0 / D, EPS, ALU.mult, ALU.add)
                dve.drain()
                V.scalar_tensor_tensor(out=var[:, :], in0=rstd[:, :], scalar=0.25, in1=var[:, :], op0=ALU.mult,
                                       op1=ALU.add)
                dve.drain()

            def over_features(numbers, t0, t1):
                return numbers[:, t0:t1].rearrange("p (t a) -> p t a", a=1).broadcast_to([P, t1 - t0, D])

            def over_tiles(row, n):
                return row.rearrange("p (a d) -> p a d", a=1).broadcast_to([P, n, D])

            def stds(n):
                dve.nop().then_inc(var_ready, 1)
                dve.wait_ge(std_ready, n)
                V.reciprocal(rstd[:, :], rstd[:, :])
                dve.drain()

            def normalised(dst, src, t):
                V.tensor_scalar(dst, src, mean[:, bass.ds(t, 1)], rstd[:, bass.ds(t, 1)], ALU.subtract, ALU.mult)
                dve.drain()

            def rectified_parts(t, h):
                V.tensor_scalar(h, h, 0.0, None, ALU.max)
                dve.drain()
                V.tensor_copy(tile4(parts, t, 0), h)
                dve.drain()
                V.tensor_tensor(tile4(parts, t, 1), h, tile4(parts, t, 0), ALU.subtract)
                dve.drain()

            norm_stats(xcur)
            stds(1)
            for half, (t0, t1) in enumerate(HALVES):
                h = x1_all[:, t0:t1, :]
                V.tensor_tensor(h, xcur[:, t0:t1, :], over_features(mean, t0, t1), ALU.subtract)
                dve.drain()
                V.scalar_tensor_tensor(out=h, in0=h, scalar=0.0, in1=over_features(rstd, t0, t1), op0=ALU.max,
                                            op1=ALU.mult).then_inc(h_made, 1)
            dve.drain()
            for half, (t0, t1) in enumerate(HALVES):
                dve.wait_ge(high_made, half + 1)
                V.tensor_tensor(parts[:, t0:t1, 1, :], x1_all[:, t0:t1, :], parts[:, t0:t1, 0, :], ALU.subtract)
            dve.drain()
            dve.nop().then_inc(h_ready, 1)
            dve.wait_ge(consts_ready, 1)
            dve.wait_ge(weights_in, DMA * 7)

            def convolve(t, m, b):
                dve.wait_ge(s_stored[b], DMA * (m + 1))
                for g, (k0, n) in enumerate(ADJ_GROUPS):
                    if g % 2 == 0:
                        dve.wait_ge(adj_flipped, t * NA + g + 9)
                        V.tensor_copy(flat(s_tile[b][:, k0:k0 + n, :]), flip_ps[0][:, :].bitcast(BF16)[:, 0:n * P]).then_inc(adj_moved_v, 1)
                dve.wait_ge(conv_done, t + 1)
                V.tensor_tensor(tile3(s_tile[b], t), tile3(s_tile[b], t), ident_bf[:, :], ALU.add).then_inc(s_made, 1)
                dve.wait_ge(proj_done, t + 1)
                V.scalar_tensor_tensor(out=tile3(x1_all, t), in0=b0_sb[:, :], scalar=row_n[:, bass.ds(t, 1)],
                                            in1=pv_ps[:, D:2 * D], op0=ALU.mult, op1=ALU.add).then_inc(proj_out, 1)
            tiles_loop(dve, convolve)

            dve.wait_ge(cols_done, 1)
            V.tensor_copy(col_n[:, :], lg[0][:, 0:NT])
            dve.drain()
            V.tensor_copy(deg_inv[:, :], col_n[:, :])
            dve.drain()
            V.tensor_tensor(deg_inv[:, NT - 1:NT], deg_inv[:, NT - 1:NT], ident[:, P - 1:P], ALU.add)
            dve.drain()
            V.reciprocal(deg_inv[:, :], deg_inv[:, :])
            for sums, inverse in ((row_n, row_inv), (col_n, col_inv)):
                V.tensor_scalar(inverse[:, :], sums[:, :], 1.0, 1e-12, ALU.add, ALU.max)
                dve.drain()
                V.reciprocal(inverse[:, :], inverse[:, :])
            dve.drain()

            V.tensor_scalar(real_row[:, :], ident[:, P - 1:P], -1.0, 1.0, ALU.mult, ALU.add)
            dve.drain()

            def first_result(t, m, b):
                V.scalar_tensor_tensor(out=tile3(x1_all, t), in0=tile3(x1_all, t), scalar=deg_inv[:, bass.ds(t, 1)],
                                       in1=tile3(xcur, t), op0=ALU.mult, op1=ALU.add)
            tiles_loop(dve, first_result)
            dve.drain()
            dve.nop().then_inc(x1_ready, 1)
            norm_stats(x1_all)
            stds(2)

            def second_norm(t, m, b):
                dve.wait_ge(first_turned, t + 1)
                normalised(ht[b][:, :], tile3(x1_all, t), t)
                rectified_parts(t, ht[b][:, :])
                V.tensor_copy(tile3(xcur, t), ht[b][:, :]).then_inc(tile_ready, 1)
            tiles_loop(dve, second_norm)
            dve.drain()
            dve.nop().then_inc(second_ready, 1)

            for s in range(2):
                def copy_logits(t, b, chunks):
                    for c in chunks:
                        c0, w = LOGIT_CHUNKS[c]
                        w = min(w, N - c0)
                        dve.wait_ge(logits_ready[s], t * NL + c + 1)
                        V.tensor_scalar(expo[b][:, c0:c0 + w], lg[c % 2][:, 0:w], 1.0, None, ALU.mult, ALU.max,
                                             accum_out=maxes[:, c:c + 1]).then_inc(logits_used[s], 1)
                    if NL - 1 not in chunks:
                        return
                    dve.drain()
                    V.tensor_reduce(out=top[:, :], in_=maxes[:, :], axis=AX.X, op=ALU.max)
                    dve.drain()
                    V.tensor_scalar(neg_max[b][:, :], top[:, :], -1.0, None, ALU.mult).then_inc(logits_copied[s], 1)

                def bisect(b, r):
                    V.scalar_tensor_tensor(out=terms[:, :], in0=expo[b][:, 0:N], scalar=cut[b][:, :].bitcast(FP32),
                                           in1=expo[b][:, 0:N], op0=ALU.is_ge, op1=ALU.mult, accum_out=mass[:, :])
                    dve.drain()
                    if r < ROUNDS[s] - 1:
                        V.tensor_scalar(move[:, :], mass[:, :], target[b][:, :], 0.5, ALU.is_ge, ALU.subtract)
                        scale = width[b][:, r + 1:r + 2]
                    else:
                        V.tensor_scalar(move[:, :], mass[:, :], target[b][:, :], None, ALU.is_ge)
                        scale = width[b][:, r + 1:r + 2]
                    dve.drain()
                    V.scalar_tensor_tensor(out=cut[b][:, :], in0=move[:, :], scalar=scale, in1=cut[b][:, :], op0=ALU.mult,
                                           op1=ALU.add)
                    dve.drain()

                def find_odd(flags, t):
                    if is_last(t):
                        V.tensor_tensor(flags, flags, real_row[:, :], ALU.mult)
                        dve.drain()
                    V.tensor_copy(odd[:, 0:1], flags)
                    dve.drain()
                    V.transpose(odd_t[:, :], odd[:, :])
                    dve.drain()
                    V.tensor_reduce(out=odd_q[:, :], in_=odd_t[:, :], axis=AX.X, op=ALU.max)
                    dve.drain()
                    for q in range(4):
                        V.tensor_copy(odd4[0:1, q:q + 1], odd_q[32 * q:32 * q + 1, :])
                    dve.drain()
                    V.tensor_reduce(out=odd_n[:, :], in_=odd4[:, :], axis=AX.X, op=ALU.max)
                    dve.drain()

                def keep_flags(b):
                    V.tensor_tensor_scan(csum[:, 1:9], ones8[:, :], top8[:, :], mass[:, :], ALU.mult, ALU.add)
                    V.tensor_copy(csum[:, 0:1], mass[:, :])
                    dve.drain()
                    V.tensor_scalar(keep8[:, :], csum[:, 0:8], target[b][:, :], None, ALU.is_lt)
                    dve.drain()

                def take_picked(b, t):
                    V.tensor_tensor(pick[:, :], top8[:, :], keep8[:, :], ALU.mult)
                    dve.drain()
                    V.tensor_reduce(out=least[:, :], in_=pick[:, :], axis=AX.X, op=ALU.add)
                    dve.drain()
                    V.scalar_tensor_tensor(out=pick[:, :], in0=keep8[:, :], scalar=-1.0, in1=pick[:, :],
                                           op0=ALU.add, op1=ALU.add)
                    V.tensor_tensor(mass[:, :], mass[:, :], least[:, :], ALU.add)
                    dve.drain()
                    V.match_replace(out=window[:, :], in_to_replace=pick[:, :], in_values=window[:, :],
                                    imm_value=-1.0)
                    V.tensor_tensor(below[:, :], mass[:, :], target[b][:, :], ALU.is_lt)
                    dve.drain()
                    find_odd(below[:, :], t)

                def step(t, m, b):
                    dve.wait_ge(expo_ready[s], t + 1)
                    for r in range(ROUNDS_SCALAR[s], ROUNDS[s]):
                        for part, chunks in enumerate((LOGITS_EARLY, LOGITS_LATE)):
                            if r == ROUNDS_SCALAR[s] + ROUNDS_BEFORE_NEXT[s][part] and not is_last(t) and chunks:
                                copy_logits(t + 1, 1 - b, chunks)
                        bisect(b, r)
                    dve.wait_ge(p_flipped[s], t * NG + 1)
                    V.scalar_tensor_tensor(out=window[:, 0:N], in0=expo[b][:, 0:N], scalar=cut[b][:, :].bitcast(FP32),
                                           in1=expo[b][:, 0:N], op0=ALU.is_lt, op1=ALU.mult, accum_out=mass[:, :])
                    dve.drain()
                    V.max(out=top8[:, :], in_=window[:, 0:N])
                    V.scalar_tensor_tensor(out=mass[:, :], in0=mass[:, :], scalar=-1.0, in1=total[b][:, :], op0=ALU.mult,
                                           op1=ALU.add)
                    dve.drain()
                    keep_flags(b)
                    V.tensor_tensor(edge[:, :], keep8[:, 0:7], keep8[:, 1:8], ALU.subtract)
                    dve.drain()
                    V.scalar_tensor_tensor(out=pick[:, 0:7], in0=edge[:, :], scalar=1.0, in1=top8[:, 0:7], op0=ALU.mult,
                                           op1=ALU.mult, accum_out=least[:, :])
                    dve.drain()
                    V.scalar_tensor_tensor(out=pick[:, 0:7], in0=edge[:, :], scalar=1.0, in1=top8[:, 1:8], op0=ALU.mult,
                                           op1=ALU.mult, accum_out=below[:, :])
                    dve.drain()
                    V.tensor_tensor(pick[:, 0:1], least[:, :], below[:, :], ALU.is_le)
                    dve.drain()
                    find_odd(pick[:, 0:1], t)
                    left = dve.alloc_register(nc.get_next_instruction_name() + "_left")
                    dve.reg_load(left, odd_n[0:1, 0:1])
                    with dve.If(dve.snap(left) < 1):
                        V.scalar_tensor_tensor(out=window[:, 0:N], in0=expo[b][:, 0:N], scalar=least[:, :],
                                               in1=expo[b][:, 0:N], op0=ALU.is_ge, op1=ALU.mult, accum_out=kept[:, :])
                        dve.drain()
                    with dve.Else():
                        take_picked(b, t)
                        dve.reg_load(left, odd_n[0:1, 0:1])
                        with dve.While(left):
                            V.max(out=top8[:, :], in_=window[:, 0:N])
                            dve.drain()
                            keep_flags(b)
                            take_picked(b, t)
                            dve.reg_load(left, odd_n[0:1, 0:1])
                        V.scalar_tensor_tensor(out=window[:, 0:N], in0=window[:, 0:N], scalar=0.0, in1=expo[b][:, 0:N],
                                               op0=ALU.max, op1=ALU.subtract, accum_out=kept[:, :])
                        dve.drain()
                    dve.end_ifs()
                    dve.wait_ge(xa_ready[s], t + 1)
                    V.reciprocal(kept_inv[b][:, :], kept[:, :]).then_inc(probs_ready[s], 1)
                    dve.drain()

                if s == 1:
                    dve.wait_ge(p_flipped[0], NT * NG + 1)
                copy_logits(0, 0, LOGITS_EARLY + LOGITS_LATE)
                tiles_loop(dve, step)

            dve.wait_ge(y_out[1], NT + 1)
            norm_stats(y_all)
            stds(3)
            tiles_loop(dve, lambda t, m, b: V.tensor_scalar(tile3(y_all, t), tile3(y_all, t), mean[:, bass.ds(t, 1)],
                                                            rstd[:, bass.ds(t, 1)], ALU.subtract, ALU.mult))
            dve.drain()
            dve.wait_ge(x1_in, DMA * 3)
            for t0, t1 in HALVES:
                y = y_all[:, t0:t1, :]
                V.tensor_tensor(y, y, over_tiles(gamma_sb, t1 - t0), ALU.mult)
                dve.drain()
                V.tensor_tensor(y, y, over_tiles(beta_sb, t1 - t0), ALU.add)
                dve.drain()
                V.tensor_tensor(xcur[:, t0:t1, :], xcur[:, t0:t1, :], y, ALU.add).then_inc(y_norm, 1)


_INS = ["x", "adj", "L0_gnn_W", "L0_gnn_b", "L1_gnn_W1", "L1_gnn_W2", "L1_gnn_W3", "L1_gnn_U1", "L1_gnn_U2",
        "L1_gnn_U3", "L1_gnn_gamma", "L1_gnn_beta"]


def kernel(**inputs):
    import numpy as np
    import concourse.bacc as bacc
    from concourse.bass_utils import run_bass_kernel_spmd

    nc = bacc.Bacc("TRN2", target_bir_lowering=False, num_devices=1)
    arrays, args = {}, []
    for name in _INS:
        a = np.ascontiguousarray(inputs[name])
        arrays[f"in_{name}"] = a
        args.append(nc.dram_tensor(f"in_{name}", a.shape, mybir.dt.from_np(a.dtype), kind="ExternalInput").ap())
    args.append(nc.dram_tensor("result", (N, D), FP32, kind="ExternalOutput").ap())
    graph_layers(nc, *args)
    r = run_bass_kernel_spmd(nc, [arrays], core_ids=[0])
    return r.results[0]["result"]
```
